# Optimizing a Trainium2 kernel written in Bass

```python
import numpy as np
import jax
import jax.numpy as jnp

def _softmax(x, axis=-1):
    return jax.nn.softmax(x, axis=axis)

def _gelu(x):
    return jax.nn.gelu(x, approximate=True)

def _silu(x):
    return jax.nn.silu(x)

def _sigmoid(x):
    return jax.nn.sigmoid(x)

def _layernorm(x, axis=-1, eps=1e-05):
    m = jnp.mean(x, axis=axis, keepdims=True)
    v = jnp.var(x, axis=axis, keepdims=True)
    return (x - m) / jnp.sqrt(v + eps)

def _scatter_add(tgt, idx, src, axis=0):
    return tgt.at[idx].add(src)

def _segment_sum(src, seg, n):
    return jax.ops.segment_sum(src, seg, n)
kernel_name = 'mk_adj_preln_d4_adj_r2_37d226'

def setup_inputs(seed: int=0):
    np.random.seed(seed)
    _w = jnp.asarray

    def _rec_inputs():
        import jax
        import jax.numpy as jnp
        _gk = jax.random.key(seed)
        x = -0.0003929 + 0.9999 * jax.random.normal(jax.random.fold_in(_gk, 1), (128, 128, 256), jnp.float32)
        _w = (1.0 + jnp.arange(128, dtype=jnp.float32)) ** (-0.5)
        _w = _w / _w.mean()
        _pij = jnp.clip(0.03125 * _w[:, None] * _w[None, :], 0.0, 1.0)
        _a = jax.random.uniform(jax.random.fold_in(_gk, 2), (128, 128, 128)) < _pij
        _a = jnp.logical_or(_a, jnp.eye(128, dtype=bool))
        _af = _a.astype(jnp.float32)
        _af = _af * jax.random.uniform(jax.random.fold_in(_gk, 3), (128, 128, 128), jnp.float32, 0.05, 1)
        adj = _af
        _nm = jnp.ones((128, 128), dtype=bool)
        nodemask = jnp.where(_nm, 1.0, 0.0).astype(jnp.float32)
        return (x, adj, nodemask)
    x, adj, nodemask = _rec_inputs()

    def _L0_gnn_setup():
        import jax, jax.numpy as jnp
        import numpy as np
        EPS = 1e-06
        key = jax.random.key(seed)
        k1, k2, k3 = jax.random.split(key, 3)
        B, N, F, O = (8, 2048, 256, 256)
        x = jax.random.normal(k1, (B, N, F), dtype=jnp.float32)
        adj = jax.random.uniform(k2, (B, N, N), dtype=jnp.float32)
        W = jax.random.normal(k3, (O, 2 * F), dtype=jnp.float32) * (1.0 / np.sqrt(2 * F))
        return {'x': x, 'adj': adj, 'W': W}
    _L0_gnn_all = _L0_gnn_setup()
    _L0_gnn_in = {k: v for k, v in _L0_gnn_all.items() if k in ('W',)}
    del _L0_gnn_all

    def _L1_gnn_setup():
        import jax, jax.numpy as jnp
        import numpy as np
        B, N, DIN, DOUT, K = (4, 1024, 256, 256, 3)
        key = jax.random.key(seed)
        ks = jax.random.split(key, 8)
        X = jax.random.normal(ks[0], (B, N, DIN), dtype=jnp.float32)
        A = jax.random.uniform(ks[1], (B, N, N), dtype=jnp.float32)
        Wv = jax.random.normal(ks[2], (DIN, DOUT), dtype=jnp.float32) * 0.02
        bv = jax.random.normal(ks[3], (DOUT,), dtype=jnp.float32) * 0.02
        aw = jax.random.normal(ks[4], (2 * DOUT, 1), dtype=jnp.float32) * 0.05
        ab = jax.random.normal(ks[5], (1,), dtype=jnp.float32) * 0.05
        Wk = jax.random.normal(ks[6], (K, DIN, DOUT), dtype=jnp.float32) * 0.02
        bk = jax.random.normal(ks[7], (K, DOUT), dtype=jnp.float32) * 0.02
        return {'X': X, 'A': A, 'Wv': Wv, 'bv': bv, 'aw': aw, 'ab': ab, 'Wk': Wk, 'bk': bk}
    _L1_gnn_all = _L1_gnn_setup()
    _L1_gnn_in = {k: v for k, v in _L1_gnn_all.items() if k in ('Wv', 'bv', 'aw', 'ab', 'Wk', 'bk')}
    del _L1_gnn_all

    def _L2_gnn_setup():
        import jax, jax.numpy as jnp
        import numpy as np
        EPS_LN = 1e-05

        def hypergraph_conv(x, adj, W, b):
            N, C, _ = adj.shape
            H = (adj != 0).astype(x.dtype)
            w = adj.reshape(N, -1)[:, :C]
            xw = jnp.einsum('ncd,hd->nch', x, W)
            Dn = jnp.einsum('nce,ne->nc', H, w)
            Dn = jnp.where(Dn > 0, 1.0 / Dn, 0.0)
            Be = H.sum(axis=1)
            Be = jnp.where(Be > 0, 1.0 / Be, 0.0)
            m = Be[:, :, None] * jnp.einsum('nce,nch->neh', H, xw)
            out = Dn[:, :, None] * jnp.einsum('nce,neh->nch', H, m)
            return out + b

        def layer_norm(x, g, b):
            mu = jnp.mean(x, axis=-1, keepdims=True)
            var = jnp.var(x, axis=-1, keepdims=True)
            return (x - mu) * jax.lax.rsqrt(var + EPS_LN) * g + b
        key = jax.random.key(seed)
        ks = jax.random.split(key, 4)
        N, C, Din, Dh, Dout = (16, 512, 256, 512, 256)
        x = jax.random.normal(ks[0], (N, C, Din), dtype=jnp.float32)
        adj = jax.random.uniform(ks[1], (N, C, C), dtype=jnp.float32, minval=0.1, maxval=1.0)
        W1 = jax.random.normal(ks[2], (Dh, Din), dtype=jnp.float32) * (1.0 / np.sqrt(Din))
        b1 = jnp.zeros((Dh,), dtype=jnp.float32)
        gamma = jnp.ones((Dh,), dtype=jnp.float32)
        beta = jnp.zeros((Dh,), dtype=jnp.float32)
        W2 = jax.random.normal(ks[3], (Dout, Dh), dtype=jnp.float32) * (1.0 / np.sqrt(Dh))
        b2 = jnp.zeros((Dout,), dtype=jnp.float32)
        return {'x': x, 'adj': adj, 'W1': W1, 'b1': b1, 'gamma': gamma, 'beta': beta, 'W2': W2, 'b2': b2}
    _L2_gnn_all = _L2_gnn_setup()
    _L2_gnn_in = {k: v for k, v in _L2_gnn_all.items() if k in ('W1', 'b1', 'gamma', 'beta', 'W2', 'b2')}
    del _L2_gnn_all

    def _L3_gnn_setup():
        import jax, jax.numpy as jnp
        import numpy as np
        B, N, IN_DIM, ATT_DIM = (2, 4096, 256, 256)
        key = jax.random.key(seed)
        k1, k2, k3, k4 = jax.random.split(key, 4)
        X = jax.random.normal(k1, (B, N, IN_DIM), dtype=jnp.float32)
        adj = jax.random.uniform(k2, (B, N, N), dtype=jnp.float32)
        mask = jnp.ones((B, N), dtype=jnp.float32)
        Wqk = jax.random.normal(k3, (IN_DIM, 2 * ATT_DIM), dtype=jnp.float32) / np.sqrt(IN_DIM)
        Wv = jax.random.normal(k4, (IN_DIM, IN_DIM), dtype=jnp.float32) / np.sqrt(IN_DIM)
        return {'X': X, 'adj': adj, 'mask': mask, 'Wqk': Wqk, 'Wv': Wv}
    _L3_gnn_all = _L3_gnn_setup()
    _L3_gnn_in = {k: v for k, v in _L3_gnn_all.items() if k in ('Wqk', 'Wv')}
    del _L3_gnn_all
    return {'x': x, 'adj': adj, 'nodemask': nodemask, 'L0_gnn_W': _L0_gnn_in['W'], 'L1_gnn_Wv': _L1_gnn_in['Wv'], 'L1_gnn_bv': _L1_gnn_in['bv'], 'L1_gnn_aw': _L1_gnn_in['aw'], 'L1_gnn_ab': _L1_gnn_in['ab'], 'L1_gnn_Wk': _L1_gnn_in['Wk'], 'L1_gnn_bk': _L1_gnn_in['bk'], 'L2_gnn_W1': _L2_gnn_in['W1'], 'L2_gnn_b1': _L2_gnn_in['b1'], 'L2_gnn_gamma': _L2_gnn_in['gamma'], 'L2_gnn_beta': _L2_gnn_in['beta'], 'L2_gnn_W2': _L2_gnn_in['W2'], 'L2_gnn_b2': _L2_gnn_in['b2'], 'L3_gnn_Wqk': _L3_gnn_in['Wqk'], 'L3_gnn_Wv': _L3_gnn_in['Wv']}

def reference(x, adj, nodemask, L0_gnn_W, L1_gnn_Wv, L1_gnn_bv, L1_gnn_aw, L1_gnn_ab, L1_gnn_Wk, L1_gnn_bk, L2_gnn_W1, L2_gnn_b1, L2_gnn_gamma, L2_gnn_beta, L2_gnn_W2, L2_gnn_b2, L3_gnn_Wqk, L3_gnn_Wv):
    import jax
    import jax.numpy as jnp

    def _L0_gnn_ref(x, adj, W):
        import jax, jax.numpy as jnp
        import numpy as np
        EPS = 1e-06
        deg = jnp.sum(adj, axis=-1, keepdims=True)
        agg = jnp.einsum('bij,bjf->bif', adj, x) / jnp.maximum(deg, EPS)
        cat = jnp.concatenate([x, agg], axis=2)
        out = jnp.einsum('bnf,of->bno', cat, W)
        return jax.nn.relu(out)

    def _L1_gnn_ref(X, A, Wv, bv, aw, ab, Wk, bk):
        import jax, jax.numpy as jnp
        import numpy as np
        B, N, DIN, DOUT, K = (4, 1024, 256, 256, 3)
        d = Wv.shape[1]
        Xw = X @ Wv + bv
        sj = Xw @ aw[:d, 0]
        si = Xw @ aw[d:, 0]
        e = jax.nn.leaky_relu(sj[:, None, :] + si[:, :, None] + ab[0], negative_slope=0.2)
        alpha_matrix = A * jnp.exp(e)
        transition = alpha_matrix / (jnp.sum(alpha_matrix, axis=-1, keepdims=True) + 1e-12)
        H = jnp.zeros(X.shape[:-1] + (d,), dtype=X.dtype)
        Xk = X
        for k in range(Wk.shape[0]):
            H = H + Xk @ Wk[k] + bk[k]
            Xk = jnp.einsum('bij,bjd->bid', transition, Xk)
        return jax.nn.relu(H)

    def _L2_gnn_ref(x, adj, W1, b1, gamma, beta, W2, b2):
        import jax, jax.numpy as jnp
        import numpy as np
        EPS_LN = 1e-05

        def hypergraph_conv(x, adj, W, b):
            N, C, _ = adj.shape
            H = (adj != 0).astype(x.dtype)
            w = adj.reshape(N, -1)[:, :C]
            xw = jnp.einsum('ncd,hd->nch', x, W)
            Dn = jnp.einsum('nce,ne->nc', H, w)
            Dn = jnp.where(Dn > 0, 1.0 / Dn, 0.0)
            Be = H.sum(axis=1)
            Be = jnp.where(Be > 0, 1.0 / Be, 0.0)
            m = Be[:, :, None] * jnp.einsum('nce,nch->neh', H, xw)
            out = Dn[:, :, None] * jnp.einsum('nce,neh->nch', H, m)
            return out + b

        def layer_norm(x, g, b):
            mu = jnp.mean(x, axis=-1, keepdims=True)
            var = jnp.var(x, axis=-1, keepdims=True)
            return (x - mu) * jax.lax.rsqrt(var + EPS_LN) * g + b
        h = jax.nn.relu(hypergraph_conv(x, adj, W1, b1))
        h = layer_norm(h, gamma, beta)
        y = hypergraph_conv(h, adj, W2, b2)
        return y + x

    def _L3_gnn_ref(X, adj, mask, Wqk, Wv):
        import jax, jax.numpy as jnp
        import numpy as np
        B, N, IN_DIM, ATT_DIM = (2, 4096, 256, 256)
        qk = X @ Wqk
        q, k = jnp.split(qk, 2, axis=-1)
        v = X @ Wv
        att_dim = q.shape[-1]
        inv_scale = 1.0 / jnp.sqrt(jnp.float32(att_dim))
        k_m = k * mask[:, :, None]
        agg = jnp.einsum('bij,bjd->bid', adj, k_m)
        w = inv_scale * mask * jnp.einsum('bid,bid->bi', q, agg)
        L = jax.nn.softmax(w, axis=1)[:, :, None] * v
        return L
    h = jnp.maximum(_layernorm(x, axis=-1), 0.0)
    x = x + _L0_gnn_ref(h, adj, L0_gnn_W)
    h = jnp.maximum(_layernorm(x, axis=-1), 0.0)
    x = x + _L1_gnn_ref(h, adj, L1_gnn_Wv, L1_gnn_bv, L1_gnn_aw, L1_gnn_ab, L1_gnn_Wk, L1_gnn_bk)
    h = jnp.maximum(_layernorm(x, axis=-1), 0.0)
    x = x + _L2_gnn_ref(h, adj, L2_gnn_W1, L2_gnn_b1, L2_gnn_gamma, L2_gnn_beta, L2_gnn_W2, L2_gnn_b2)
    h = jnp.maximum(_layernorm(x, axis=-1), 0.0)
    x = x + _L3_gnn_ref(h, adj, nodemask, L3_gnn_Wqk, L3_gnn_Wv)
    return x

_drawn_inputs = setup_inputs


def setup_inputs(seed=0):
    import zlib

    import numpy as np

    out = dict(_drawn_inputs(seed))
    spreads = {'L2_gnn_b1': (0.0, 0.1),
     'L2_gnn_gamma': (1.0, 0.2),
     'L2_gnn_beta': (0.0, 0.1),
     'L2_gnn_b2': (0.0, 0.8)}
    factors = {'L1_gnn_Wv': 8.0, 'L1_gnn_bv': 64.0, 'L1_gnn_aw': 8.0, 'L3_gnn_Wqk': 8.0, 'L3_gnn_Wv': 8.0}
    for name, (base, spread) in spreads.items():
        noise = np.random.default_rng([zlib.crc32(name.encode()), seed]).standard_normal(out[name].shape)
        drawn = base * np.exp(spread * noise) if base else spread * noise
        out[name] = jnp.asarray(drawn.astype(out[name].dtype))
    for name, factor in factors.items():
        out[name] = (out[name] * factor).astype(out[name].dtype)
    return out
```

```python
from contextlib import ExitStack

import concourse.bass as bass
from concourse import mybir

F32 = mybir.dt.float32
F32R = mybir.dt.float32r
ALU = mybir.AluOpType
ACT = mybir.ActivationFunctionType
AX = mybir.AxisListType

P = 128
SLOTS = 4
EPS = 1e-5
DEPTH = 5

FIRST_LOOP_STEP = 8


class Graph:

    def __init__(self, n, s):
        self.n = n
        self.s = s
        self.s2 = s % 2


def in_flight(t, k, back, graphs):
    if isinstance(t, int) and not 0 <= t - back < graphs:
        return None
    return Graph(t - back, (k - back) % SLOTS)


def wait(eng, sem, count):
    if not isinstance(count, int) or count > 0:
        eng.wait_ge(sem, count)


def constant_wait(eng, sem):
    eng.wait_ge(sem, 1)


def run_steps(eng, step, graphs):
    for t in range(FIRST_LOOP_STEP):
        step(t, t % SLOTS)
    with eng.Fori(FIRST_LOOP_STEP, graphs - SLOTS + 1, SLOTS) as t0:
        for k in range(SLOTS):
            step(t0 + k, k)
    for t in range(graphs, graphs + DEPTH + 1):
        step(t, t % SLOTS)


def build(nc, x, adj, mask_t, w0t, wk, w1t, w2t, wv3, wqk_t, wv1t, aw, bv, ab, bk, b1, b2, gamma, beta, out):
    G, N, F = x.shape
    FC = F // P
    H = w1t.shape[1]
    HC = H // P
    K = bk.shape[0]
    assert N == P and F == 2 * P and H == 2 * F and K == 3 and (G - FIRST_LOOP_STEP) % SLOTS == 0
    SCORE_SCALE = float(F) ** -0.5

    with ExitStack() as ctx:
        def sb(name, shape, dt=F32):
            return ctx.enter_context(nc.sbuf_tensor(name, shape, dt))

        def sem(name):
            return ctx.enter_context(nc.semaphore(name))

        parts = [("gate0", FC * 2 * F), ("k10", FC * 2 * F), ("k2u", FC * (F + 2)),
                 ("w1", FC * H), ("w2", HC * F), ("mv", FC * 2 * F)]
        at, col = {}, 0
        for name, width in parts:
            at[name] = (col, col + width)
            col += width
        w32 = sb("w32", [P, col])
        w_hi = sb("w_hi", [P, col], F32R)
        w_lo = sb("w_lo", [P, col], F32R)

        def weight(tile, name, chunks):
            return tile[:, at[name][0]:at[name][1]].rearrange("p (c n) -> p c n", c=chunks)

        gate0 = [weight(w, "gate0", FC) for w in (w32, w_hi, w_lo)]
        k10 = [weight(w, "k10", FC) for w in (w32, w_hi, w_lo)]
        k2u = [weight(w, "k2u", FC) for w in (w32, w_hi, w_lo)]
        w1 = [weight(w, "w1", FC) for w in (w32, w_hi, w_lo)]
        w2 = [weight(w, "w2", HC) for w in (w32, w_hi, w_lo)]
        mv = [weight(w, "mv", FC) for w in (w32, w_hi, w_lo)]

        w2_raw = sb("w2_raw", [P, HC, F])
        wqk_sb = sb("wqk_sb", [P, 2 * FC, F])
        wv1_sb = sb("wv1_sb", [P, FC, F])
        aw_sb = sb("aw_sb", [P, FC, 2])
        bv_sb = sb("bv_sb", [P, FC])
        gamma_sb = sb("gamma_sb", [P, HC])
        beta_sb = sb("beta_sb", [P, HC])
        ab_sb = sb("ab_sb", [P, 1])
        bk3 = sb("bk3", [P, K, F])
        bk_sum = sb("bk_sum", [P, F])
        bk_hi = sb("bk_hi", [P, F], F32R)
        bias_rows = sb("bias_rows", [P, F], F32R)
        spread32 = sb("spread32", [P, P])
        spread = sb("spread", [P, P], F32R)
        b1_rows = sb("b1_rows", [P, H])
        b2_rows = sb("b2_rows", [P, F])
        beta_w2 = sb("beta_w2", [P, F])
        score_bias = sb("score_bias", [P, 1])
        mask_sb = sb("mask_sb", [P, G])
        mask_scaled = sb("mask_scaled", [P, G])
        ident = sb("ident", [P, P])
        minus_half = sb("minus_half", [P, 1])

        x_in = sb("x_in", [P, SLOTS, F])
        adj_in = sb("adj_in", [P, SLOTS, N])
        stats = {n: sb(f"stats_{n}", [P, 6]) for n in range(5)}
        mean_var = {n: sb(f"mean_var_{n}", [P, 2, 2]) for n in range(5)}
        var_eps = {n: sb(f"var_eps_{n}", [P, 1]) for n in range(5)}
        rstd = {n: sb(f"rstd_{n}", [P, 2]) for n in range(5)}
        shift = {n: sb(f"shift_{n}", [P, 2]) for n in range(5)}
        deg = sb("deg", [P, 1])
        deg_max = sb("deg_max", [P, 1])
        deg_inv = sb("deg_inv", [P, 2])
        adj_norm = sb("adj_norm", [P, 2, N])
        h0 = sb("h0", [P, 2, F])
        adjm_t = sb("adjm_t", [P, SLOTS, N])
        adjn_t = sb("adjn_t", [P, 2, N])
        h0t_hi = sb("h0t_hi", [P, F], F32R)
        h0t_lo = sb("h0t_lo", [P, F], F32R)
        inc_t = sb("inc_t", [P, 2, N], F32R)
        edge_size = sb("edge_size", [P, 1])
        edge_w = sb("edge_w", [P, 2, 1])
        b_inv = sb("b_inv", [P, 2, 1])
        b_hi = sb("b_hi", [P, 1], F32R)
        b_lo = sb("b_lo", [P, 1])
        binc_hi = sb("binc_hi", [P, 2, N], F32R)
        binc_lo = sb("binc_lo", [P, 2, N], F32R)
        ones_col = sb("ones_col", [P, 2])
        gb = sb("gb", [P, F])
        s_mat = sb("s_mat", [P, SLOTS, N])
        node_sum = sb("node_sum", [P, 2])
        d_max = sb("d_max", [P, 1])
        d_rec = sb("d_rec", [P, 1])
        d_inv = sb("d_inv", [P, SLOTS])
        rho = sb("rho", [P, SLOTS])
        x1 = sb("x1", [P, SLOTS, F])
        h1 = sb("h1", [P, F])
        h1t_hi = sb("h1t_hi", [P, F], F32R)
        h1t_lo = sb("h1t_lo", [P, F], F32R)
        g2s = sb("g2s", [P, F + 2])
        si = sb("si", [P, 2])
        z_max = sb("z_max", [P, N])
        z_exp = sb("z_exp", [P, N])
        alpha = sb("alpha", [P, N])
        row_sum = sb("row_sum", [P, 1])
        row_eps = sb("row_eps", [P, 1])
        row_inv = sb("row_inv", [P, 1])
        trans = sb("trans", [P, N])
        trans_t = sb("trans_t", [P, N])
        q1 = sb("q1", [P, F])
        x2 = sb("x2", [P, 2, F])
        x2b = sb("x2b", [P, F])
        h2 = sb("h2", [P, 2, F])
        base_h = sb("base_h", [P, F])
        base_r = sb("base_r", [P, F])
        base = sb("base", [P, 2, F])
        sh_hi = sb("sh_hi", [P, F], F32R)
        sh_lo = sb("sh_lo", [P, F], F32R)
        r0 = sb("r0", [P, H])
        r1 = sb("r1", [P, H])
        zn = sb("zn", [P, H])
        sz_hi = sb("sz_hi", [P, H], F32R)
        sz_lo = sb("sz_lo", [P, H], F32R)
        x3 = sb("x3", [P, 2, F])
        h3 = sb("h3", [P, 2, F])
        h3t_hi = sb("h3t_hi", [P, F], F32R)
        h3t_lo = sb("h3t_lo", [P, F], F32R)
        t32 = sb("t32", [P, F])
        prod = sb("prod", [P, F])
        w_raw = sb("w_raw", [P, 1])
        w_col = sb("w_col", [P, 1])
        neg_max = sb("neg_max", [P, 1])
        e_row = sb("e_row", [P, N])
        e_sum = sb("e_sum", [P, 1])
        e_col = sb("e_col", [P, 1])
        e_inv = sb("e_inv", [P, 1])
        p_col = sb("p_col", [P, 1])
        y = sb("y", [P, 2, F])

        bank = [ctx.enter_context(nc.psum_tensor(f"bank{n}", [P, 512], F32)) for n in range(8)]
        A0, B0, A1, B1, A2, B2, A3, B3 = bank

        (weights_in, ident_zero, ident_done, consts_done, setup_products, setup_evacuated,
         w32_done, w_hi_done, bias_summed, bias_hi_done, weights_ready) = [sem(n) for n in (
             "weights_in", "ident_zero", "ident_done", "consts_done", "setup_products",
             "setup_evacuated", "w32_done", "w_hi_done", "bias_summed", "bias_hi_done",
             "weights_ready")]
        x_loaded = [sem(f"x_loaded{i}") for i in range(SLOTS)]
        adj_loaded = [sem(f"adj_loaded{i}") for i in range(SLOTS)]
        y_stored = [sem(f"y_stored{i}") for i in range(2)]
        stats_done = [sem(f"stats_done{i}") for i in range(5)]
        aggr_done = [sem(f"aggr_done{i}") for i in range(5)]
        var_done = [sem(f"var_done{i}") for i in range(5)]
        rstd_done = [sem(f"rstd_done{i}") for i in range(5)]
        shift_done = [sem(f"shift_done{i}") for i in range(5)]
        names = """deg_done deg_clamped deg_ready adjn_done h0_done l0_transposed l0_copied inc_done
            binv_clamped binv_done bhi_done blo_done binc_done l0_split gates_done gb_copied
            s_done s_copied sums_copied dclamp_done drec_done dinv_done d_done agg_done x1_done h1_done
            h1_transposed h1_hi_done h1_split g2s_done g10_done g2s_copied si_done sj_spread
            exp_max_done exp_done alpha_done row_eps_done row_inv_done trans_done trans_transposed
            trans_copied hop1_done q1_done hop2_done x2_done h2_done x2b_done base_h_done
            base_r_done base_done sh_done sh_hi_done sh_split w1_done r0_done r1_done zn_done
            sz_done sz_hi_done sz_split w2_done x3_done h3_done h3_transposed h3_hi_done h3_split
            agg3_done tv_done t_copied w_raw_done w_done w_spread max_done e_row_done e_col_done
            e_inv_done p_done y_done""".split()
        S = {n: sem(n) for n in names}
        (deg_done, deg_clamped, deg_ready, adjn_done, h0_done, l0_transposed, l0_copied, inc_done,
         binv_clamped, binv_done, bhi_done, blo_done, binc_done, l0_split, gates_done, gb_copied,
         s_done, s_copied, sums_copied, dclamp_done, drec_done, dinv_done, d_done, agg_done, x1_done, h1_done,
         h1_transposed, h1_hi_done, h1_split, g2s_done, g10_done, g2s_copied, si_done, sj_spread,
         exp_max_done, exp_done, alpha_done, row_eps_done, row_inv_done, trans_done, trans_transposed,
         trans_copied, hop1_done, q1_done, hop2_done, x2_done, h2_done, x2b_done, base_h_done,
         base_r_done, base_done, sh_done, sh_hi_done, sh_split, w1_done, r0_done, r1_done, zn_done,
         sz_done, sz_hi_done, sz_split, w2_done, x3_done, h3_done, h3_transposed, h3_hi_done,
         h3_split, agg3_done, tv_done, t_copied, w_raw_done, w_done, w_spread, max_done, e_row_done,
         e_col_done, e_inv_done, p_done, y_done) = [S[n] for n in names]

        def loaded(eng, sems, g):
            count = ((g.n - g.s) // SLOTS + 1) * 16 if isinstance(g.n, int) else (g.n - g.s) * 4 + 16
            eng.wait_ge(sems[g.s], count)

        block = ctx.enter_context(nc.Block())

        @block.sync
        def _(sp):
            def c(ap, chunks):
                return ap.rearrange("(c p) n -> p c n", c=chunks)

            for dst, src in (
                (gate0[0][:, :, 0:F], c(w0t[F:2 * F, :], FC)), (gate0[0][:, :, F:2 * F], c(w0t[0:F, :], FC)),
                (k10[0][:, :, 0:F], c(wk[1], FC)), (k10[0][:, :, F:2 * F], c(wk[0], FC)),
                (k2u[0][:, :, 0:F], c(wk[2], FC)), (w1[0], c(w1t, FC)), (w2_raw[:], c(w2t, HC)),
                (mv[0][:, :, F:2 * F], c(wv3, FC)), (wqk_sb[:], c(wqk_t, 2 * FC)),
                (wv1_sb[:], c(wv1t, FC)), (aw_sb[:], aw), (bv_sb[:], bv), (gamma_sb[:], gamma),
                (beta_sb[:], beta), (mask_sb[:], mask_t),
                (ab_sb[:], ab.rearrange("(a n) -> a n", a=1).to_broadcast([P, 1])),
                (b1_rows[:], b1.rearrange("(a n) -> a n", a=1).to_broadcast([P, H])),
                (b2_rows[:], b2.rearrange("(a n) -> a n", a=1).to_broadcast([P, F])),
            ):
                sp.dma_start(dst, src).then_inc(weights_in, 16)
            for k in range(K):
                sp.dma_start(bk3[:, k, :], bk[k:k + 1, :].to_broadcast([P, F])).then_inc(weights_in, 16)

            def load(g):
                wait(sp, x1_done, g.n - SLOTS + 1)
                sp.dma_start(x_in[:, g.s, :], x[g.n]).then_inc(x_loaded[g.s], 16)
                wait(sp, inc_done, g.n - SLOTS + 1)
                wait(sp, alpha_done, g.n - SLOTS + 1)
                sp.dma_start(adj_in[:, g.s, :], adj[g.n]).then_inc(adj_loaded[g.s], 16)

            def store(g):
                wait(sp, y_done, g.n + 1)
                sp.dma_start(out[g.n], y[:, g.s2, :]).then_inc(y_stored[g.s2], 16)

            def step(t, k):
                if (g := in_flight(t, k, 0, G)):
                    load(g)
                if (g := in_flight(t, k, DEPTH + 1, G)):
                    store(g)

            run_steps(sp, step, G)
            for i in range(2):
                sp.wait_ge(y_stored[i], 16 * G // 2)

        WEIGHT_LOADS = 18 + K

        @block.gpsimd
        def _(pool):
            pool.memset(minus_half[:], -0.5)
            pool.memset(ones_col[:], 1.0)
            pool.memset(spread32[:], 2.0 / P).then_inc(consts_done, 1)
            pool.memset(ident[:], 0.0).then_inc(ident_zero, 1)
            pool.wait_ge(ident_zero, 1)
            pool.affine_select(out=ident[:], in_=ident[:], compare_op=ALU.not_equal, fill=1.0, base=0,
                               pattern=[[-1, P]], channel_multiplier=1).then_inc(ident_done, 1)
            pool.wait_ge(consts_done, 1)
            pool.wait_ge(weights_ready, 1)

            def norm(n, g, used, with_shift=True):
                wait(pool, used, g.n - 1)
                pool.wait_ge(var_done[n], g.n + 1)
                r = rstd[n][:, g.s2:g.s2 + 1]
                pool.tensor_tensor(r, var_eps[n][:], minus_half[:], ALU.pow).then_inc(rstd_done[n], 1)
                if with_shift:
                    constant_wait(pool, consts_done)
                    pool.wait_ge(rstd_done[n], g.n + 1)
                    pool.tensor_scalar(shift[n][:, g.s2:g.s2 + 1], mean_var[n][:, g.s2, 0:1], r, -1.0,
                                       ALU.mult, ALU.mult).then_inc(shift_done[n], 1)

            def residual(g):
                pool.wait_ge(x2_done, g.n + 1)
                wait(pool, base_h_done, g.n)
                pool.tensor_tensor(x2b[:], x2[:, g.s2, :], b2_rows[:], ALU.add).then_inc(x2b_done, 1)
                constant_wait(pool, consts_done)
                pool.wait_ge(d_done, g.n + 1)
                wait(pool, base_done, g.n)
                pool.tensor_scalar(base_r[:], beta_w2[:], rho[:, g.s:g.s + 1], 1.0, ALU.mult, ALU.mult)\
                    .then_inc(base_r_done, 1)
                pool.wait_ge(h2_done, g.n + 1)
                pool.wait_ge(x2b_done, g.n + 1)
                pool.tensor_tensor(base_h[:], x2b[:], h2[:, g.s2, :], ALU.add).then_inc(base_h_done, 1)
                pool.wait_ge(base_h_done, g.n + 1)
                pool.wait_ge(base_r_done, g.n + 1)
                wait(pool, x3_done, g.n - 1)
                pool.tensor_tensor(base[:, g.s2, :], base_h[:], base_r[:], ALU.add).then_inc(base_done, 1)

            def step(t, k):
                if (g := in_flight(t, k, 3, G)):
                    norm(2, g, h2_done)
                if (g := in_flight(t, k, 4, G)):
                    norm(4, g, zn_done, with_shift=False)
                if (g := in_flight(t, k, 0, G)):
                    norm(0, g, h0_done)
                if (g := in_flight(t, k, 3, G)):
                    residual(g)
                if (g := in_flight(t, k, 4, G)):
                    norm(3, g, h3_done)
                if (g := in_flight(t, k, 1, G)):
                    norm(1, g, h1_done)

            run_steps(pool, step, G)

        @block.scalar
        def _(act):
            act.wait_ge(weights_in, 16 * WEIGHT_LOADS)
            act.wait_ge(w32_done, 1)
            act.activation(w_hi[:], w32[:], ACT.Copy).then_inc(w_hi_done, 1)
            act.wait_ge(bias_summed, 2)
            act.activation(bk_hi[:], bk_sum[:], ACT.Copy).then_inc(bias_hi_done, 1)
            act.wait_ge(consts_done, 1)
            act.activation(spread[:], spread32[:], ACT.Copy).then_inc(weights_ready, 1)

            def relu_norm(n, g, dst, src, done):
                act.wait_ge(shift_done[n], g.n + 1)
                act.activation(dst, src, ACT.Relu, bias=shift[n][:, g.s2:g.s2 + 1],
                               scale=rstd[n][:, g.s2:g.s2 + 1]).then_inc(done, 1)

            def norm0(g):
                act.wait_ge(deg_ready, g.n + 1)
                wait(act, l0_transposed, g.n - 1)
                act.activation(adj_norm[:, g.s2, :], adj_in[:, g.s, :], ACT.Copy,
                               scale=deg_inv[:, g.s2:g.s2 + 1]).then_inc(adjn_done, 1)
                relu_norm(0, g, h0[:, g.s2, :], x_in[:, g.s, :], h0_done)

            def l0_copies(g):
                act.wait_ge(l0_transposed, g.n + 1)
                wait(act, agg3_done, g.n - SLOTS + 1)
                wait(act, sums_copied, g.n - 1)
                act.activation(adjm_t[:, g.s, :], A0[:, 0:N], ACT.Copy,
                               scale=mask_sb[:, bass.ds(g.n, 1)])
                act.activation(adjn_t[:, g.s2, :], A0[:, N:2 * N], ACT.Copy)
                act.activation(edge_w[:, g.s2, :], A0[:, 0:1], ACT.Copy)
                act.activation(h0t_hi[:], A0[:, 2 * N:2 * N + F], ACT.Copy).then_inc(l0_copied, 1)

            def gb_copy(g):
                act.wait_ge(gates_done, g.n + 1)
                act.activation(gb[:], B0[:, 0:F], ACT.Copy).then_inc(gb_copied, 1)

            def s_copy(g):
                act.wait_ge(s_done, g.n + 1)
                wait(act, sz_done, g.n - SLOTS + 1)
                wait(act, dclamp_done, g.n)
                wait(act, d_done, g.n)
                act.activation(s_mat[:, g.s, :], A0[:, 0:N], ACT.Copy).then_inc(s_copied, 1)
                act.activation(node_sum[:], A0[:, N:N + 4:2], ACT.Copy).then_inc(sums_copied, 1)

            def norm1(g):
                wait(act, h1_transposed, g.n)
                relu_norm(1, g, h1[:], x1[:, g.s, :], h1_done)

            def h1_hi(g):
                act.wait_ge(h1_transposed, g.n + 1)
                act.activation(h1t_hi[:], A1[:, 0:F], ACT.Copy).then_inc(h1_hi_done, 1)

            def g2s_copy(g):
                act.wait_ge(g2s_done, g.n + 1)
                act.activation(g2s[:], B1[:, 0:F + 2], ACT.Copy).then_inc(g2s_copied, 1)

            def scores(g):
                act.wait_ge(sj_spread, g.n + 1)
                act.wait_ge(si_done, g.n + 1)
                wait(act, exp_max_done, g.n)
                act.activation(z_exp[:], B1[:, 0:N], ACT.Exp, bias=si[:, 0:1])
                act.activation(B1[:, N:2 * N], B1[:, 0:N], ACT.Exp, bias=si[:, 1:2], scale=0.2)\
                    .then_inc(exp_done, 1)

            def trans_copy(g):
                act.wait_ge(trans_transposed, g.n + 1)
                act.activation(trans_t[:], B1[:, 0:N], ACT.Copy).then_inc(trans_copied, 1)

            def q1_copy(g):
                act.wait_ge(hop1_done, g.n + 1)
                act.activation(q1[:], A1[:, 0:F], ACT.Copy).then_inc(q1_done, 1)

            def norm2(g):
                wait(act, sh_done, g.n - 1)
                wait(act, base_h_done, g.n - 1)
                relu_norm(2, g, h2[:, g.s2, :], x2[:, g.s2, :], h2_done)

            def sh_hi_copy(g):
                act.wait_ge(sh_done, g.n + 1)
                act.activation(sh_hi[:], A2[:, 0:F], ACT.Copy).then_inc(sh_hi_done, 1)

            def hidden_relu(g):
                act.wait_ge(r0_done, g.n + 1)
                wait(act, zn_done, g.n)
                act.activation(r1[:], r0[:], ACT.Relu).then_inc(r1_done, 1)

            def sz_hi_copy(g):
                act.wait_ge(sz_done, g.n + 1)
                act.activation(sz_hi[:], A2[:, 0:H], ACT.Copy).then_inc(sz_hi_done, 1)

            def norm3(g):
                wait(act, agg3_done, g.n - 1)
                relu_norm(3, g, h3[:, g.s2, :], x3[:, g.s2, :], h3_done)

            def h3_hi(g):
                act.wait_ge(h3_transposed, g.n + 1)
                act.activation(h3t_hi[:], A3[:, 0:F], ACT.Copy).then_inc(h3_hi_done, 1)

            def t_copy(g):
                act.wait_ge(tv_done, g.n + 1)
                wait(act, w_raw_done, g.n)
                act.activation(t32[:], B3[:, 0:F], ACT.Copy).then_inc(t_copied, 1)

            def softmax(g):
                act.wait_ge(max_done, g.n + 1)
                wait(act, p_done, g.n)
                act.activation(e_row[:], A3[:, 0:N], ACT.Exp, bias=neg_max[:], accum_out=e_sum[:])\
                    .then_inc(e_row_done, 1)
                act.activation(e_col[:], w_col[:], ACT.Exp, bias=neg_max[:]).then_inc(e_col_done, 1)

            def step(t, k):
                if (g := in_flight(t, k, 2, G)):
                    h1_hi(g)
                if (g := in_flight(t, k, 4, G)):
                    hidden_relu(g)
                if (g := in_flight(t, k, 1, G)):
                    l0_copies(g)
                if (g := in_flight(t, k, 5, G)):
                    t_copy(g)
                if (g := in_flight(t, k, 3, G)):
                    norm2(g)
                if (g := in_flight(t, k, 2, G)):
                    g2s_copy(g)
                if (g := in_flight(t, k, 4, G)):
                    sz_hi_copy(g)
                if (g := in_flight(t, k, 0, G)):
                    norm0(g)
                if (g := in_flight(t, k, 1, G)):
                    gb_copy(g)
                if (g := in_flight(t, k, 3, G)):
                    sh_hi_copy(g)
                if (g := in_flight(t, k, 2, G)):
                    scores(g)
                if (g := in_flight(t, k, 1, G)):
                    s_copy(g)
                if (g := in_flight(t, k, 5, G)):
                    softmax(g)
                if (g := in_flight(t, k, 2, G)):
                    trans_copy(g)
                    q1_copy(g)
                if (g := in_flight(t, k, 4, G)):
                    norm3(g)
                if (g := in_flight(t, k, 1, G)):
                    norm1(g)
                if (g := in_flight(t, k, 4, G)):
                    h3_hi(g)

            run_steps(act, step, G)

        @block.vector
        def _(dve):
            dve.wait_ge(weights_in, 16 * WEIGHT_LOADS)
            dve.tensor_scalar(mask_scaled[:], mask_sb[:], SCORE_SCALE, None, ALU.mult)
            for c in range(HC):
                dve.tensor_scalar(w2[0][:, c, :], w2_raw[:, c, :], gamma_sb[:, c:c + 1], None, ALU.mult)
            dve.tensor_tensor(bk_sum[:], bk3[:, 0, :], bk3[:, 1, :], ALU.add).then_inc(bias_summed, 1)
            dve.wait_ge(bias_summed, 1)
            dve.tensor_tensor(bk_sum[:], bk_sum[:], bk3[:, 2, :], ALU.add).then_inc(bias_summed, 1)
            dve.wait_ge(setup_products, 1)
            dve.tensor_copy(mv[0][:, :, 0:F], A0[:].rearrange("p (c n) -> p c n", c=FC))
            dve.tensor_copy(k2u[0][:, :, F:F + 2], B0[:, 0:2 * FC].rearrange("p (c n) -> p c n", c=FC))\
                .then_inc(w32_done, 1)
            dve.tensor_tensor(score_bias[:], A1[:, 0:1], ab_sb[:], ALU.add)
            dve.tensor_copy(beta_w2[:], B1[:, 0:F]).then_inc(setup_evacuated, 1)
            dve.wait_ge(w_hi_done, 1)
            dve.tensor_tensor(w_lo[:], w32[:], w_hi[:].bitcast(F32), ALU.subtract)
            dve.wait_ge(bias_hi_done, 1)
            dve.tensor_copy(bias_rows[0:P // 2, :], bk_hi[0:P // 2, :].bitcast(F32))
            dve.tensor_tensor(bias_rows[P // 2:P, :], bk_sum[P // 2:P, :], bk_hi[P // 2:P, :].bitcast(F32),
                              ALU.subtract).then_inc(weights_ready, 1)
            dve.wait_ge(setup_evacuated, 1)

            def norm_stats(n, g, src, rstd_used=None):
                dve.bn_stats(stats[n][:], src).then_inc(stats_done[n], 1)
                constant_wait(dve, weights_ready)
                dve.wait_ge(stats_done[n], g.n + 1)
                if rstd_used is not None:
                    wait(dve, rstd_used, g.n - 1)
                dve.bn_aggr(mean_var[n][:, g.s2, :], stats[n][:]).then_inc(aggr_done[n], 1)
                dve.wait_ge(aggr_done[n], g.n + 1)
                wait(dve, rstd_done[n], g.n)
                dve.tensor_scalar(var_eps[n][:], mean_var[n][:, g.s2, 1:2], EPS, None, ALU.add)\
                    .then_inc(var_done[n], 1)

            def norm0(g):
                loaded(dve, adj_loaded, g)
                dve.tensor_reduce(deg[:], adj_in[:, g.s, :], AX.X, ALU.add).then_inc(deg_done, 1)
                dve.wait_ge(deg_done, g.n + 1)
                dve.tensor_scalar(deg_max[:], deg[:], 1e-6, None, ALU.max).then_inc(deg_clamped, 1)
                dve.wait_ge(deg_clamped, g.n + 1)
                wait(dve, adjn_done, g.n - 1)
                dve.reciprocal(deg_inv[:, g.s2:g.s2 + 1], deg_max[:]).then_inc(deg_ready, 1)
                loaded(dve, x_loaded, g)
                norm_stats(0, g, x_in[:, g.s, :], shift_done[0])

            def l0_split_(g):
                dve.wait_ge(l0_copied, g.n + 1)
                dve.tensor_tensor(h0t_lo[:], A0[:, 2 * N:2 * N + F], h0t_hi[:].bitcast(F32), ALU.subtract)\
                    .then_inc(l0_split, 1)
                wait(dve, s_done, g.n - 1)
                dve.tensor_scalar(inc_t[:, g.s2, :], A0[:, 0:N], 0.0, None, ALU.not_equal, ALU.add,
                                  accum_out=edge_size[:]).then_inc(inc_done, 1)

            def edges(g):
                dve.wait_ge(inc_done, g.n + 1)
                dve.tensor_scalar(edge_size[:], edge_size[:], 1.0, None, ALU.max).then_inc(binv_clamped, 1)
                dve.wait_ge(binv_clamped, g.n + 1)
                dve.reciprocal(b_inv[:, 0, :], edge_size[:]).then_inc(binv_done, 1)
                dve.wait_ge(binv_done, g.n + 1)
                dve.tensor_copy(b_hi[:], b_inv[:, 0, :]).then_inc(bhi_done, 1)
                dve.wait_ge(bhi_done, g.n + 1)
                dve.tensor_tensor(b_lo[:], b_inv[:, 0, :], b_hi[:].bitcast(F32), ALU.subtract)\
                    .then_inc(blo_done, 1)
                dve.tensor_scalar(binc_hi[:, g.s2, :], inc_t[:, g.s2, :].bitcast(F32), b_hi[:].bitcast(F32),
                                  None, ALU.mult)
                dve.wait_ge(blo_done, g.n + 1)
                dve.tensor_scalar(binc_lo[:, g.s2, :], inc_t[:, g.s2, :].bitcast(F32), b_lo[:],
                                  None, ALU.mult).then_inc(binc_done, 1)

            def node_degrees(g):
                dve.wait_ge(sums_copied, g.n + 1)
                dve.tensor_scalar(d_max[:], node_sum[:, 0:1], 1.1754944e-38, None, ALU.max)\
                    .then_inc(dclamp_done, 1)
                dve.wait_ge(dclamp_done, g.n + 1)
                dve.reciprocal(d_rec[:], d_max[:]).then_inc(drec_done, 1)
                dve.wait_ge(drec_done, g.n + 1)
                wait(dve, x3_done, g.n - SLOTS + 1)
                wait(dve, base_r_done, g.n - SLOTS + 1)
                dve.scalar_tensor_tensor(d_inv[:, g.s:g.s + 1], node_sum[:, 0:1], 0.0, d_rec[:],
                                         ALU.is_gt, ALU.mult).then_inc(dinv_done, 1)
                dve.wait_ge(dinv_done, g.n + 1)
                dve.tensor_tensor(rho[:, g.s:g.s + 1], node_sum[:, 1:2], d_inv[:, g.s:g.s + 1], ALU.mult)\
                    .then_inc(d_done, 1)

            def x1_sum(g):
                dve.wait_ge(agg_done, g.n + 1)
                loaded(dve, x_loaded, g)
                dve.scalar_tensor_tensor(x1[:, g.s, :], B0[:, F:2 * F], 0.0, x_in[:, g.s, :],
                                         ALU.max, ALU.add).then_inc(x1_done, 1)
                dve.wait_ge(x1_done, g.n + 1)
                norm_stats(1, g, x1[:, g.s, :], shift_done[1])

            def h1_lo(g):
                dve.wait_ge(h1_hi_done, g.n + 1)
                dve.tensor_tensor(h1t_lo[:], A1[:, 0:F], h1t_hi[:].bitcast(F32), ALU.subtract)\
                    .then_inc(h1_split, 1)

            def si_add(g):
                dve.wait_ge(g2s_copied, g.n + 1)
                wait(dve, exp_done, g.n)
                dve.tensor_scalar(si[:, 0:1], g2s[:, F + 1:F + 2], score_bias[:], None, ALU.add)
                dve.tensor_scalar(si[:, 1:2], g2s[:, F + 1:F + 2], score_bias[:], 0.2, ALU.add, ALU.mult)\
                    .then_inc(si_done, 1)

            def transition(g):
                dve.wait_ge(exp_done, g.n + 1)
                dve.tensor_tensor(z_max[:], B1[:, N:2 * N], z_exp[:], ALU.max).then_inc(exp_max_done, 1)
                dve.wait_ge(exp_max_done, g.n + 1)
                dve.tensor_tensor_reduce(alpha[:], z_max[:], adj_in[:, g.s, :], 1.0, 0.0, ALU.mult,
                                         ALU.add, row_sum[:]).then_inc(alpha_done, 1)
                dve.wait_ge(alpha_done, g.n + 1)
                dve.tensor_scalar(row_eps[:], row_sum[:], 1e-12, None, ALU.add).then_inc(row_eps_done, 1)
                dve.wait_ge(row_eps_done, g.n + 1)
                dve.reciprocal(row_inv[:], row_eps[:]).then_inc(row_inv_done, 1)
                dve.wait_ge(row_inv_done, g.n + 1)
                wait(dve, trans_transposed, g.n)
                dve.tensor_scalar(trans[:], alpha[:], row_inv[:], None, ALU.mult).then_inc(trans_done, 1)

            def x2_sum(g):
                dve.wait_ge(hop2_done, g.n + 1)
                wait(dve, h2_done, g.n - 1)
                wait(dve, x2b_done, g.n - 1)
                dve.scalar_tensor_tensor(x2[:, g.s2, :], A1[:, F:2 * F], 0.0, x1[:, g.s, :],
                                         ALU.max, ALU.add).then_inc(x2_done, 1)
                dve.wait_ge(x2_done, g.n + 1)
                norm_stats(2, g, x2[:, g.s2, :], shift_done[2])

            def sh_lo_part(g):
                dve.wait_ge(sh_hi_done, g.n + 1)
                dve.tensor_tensor(sh_lo[:], A2[:, 0:F], sh_hi[:].bitcast(F32), ALU.subtract)\
                    .then_inc(sh_split, 1)

            def hidden(g):
                dve.wait_ge(w1_done, g.n + 1)
                wait(dve, r1_done, g.n)
                dve.scalar_tensor_tensor(r0[:], B2[:, 0:H], d_inv[:, g.s:g.s + 1], b1_rows[:],
                                         ALU.mult, ALU.add).then_inc(r0_done, 1)

            def hidden_norm(g):
                dve.wait_ge(r1_done, g.n + 1)
                norm_stats(4, g, r1[:])
                dve.wait_ge(rstd_done[4], g.n + 1)
                wait(dve, sz_done, g.n)
                dve.tensor_scalar(zn[:], r1[:], mean_var[4][:, g.s2, 0:1], rstd[4][:, g.s2:g.s2 + 1],
                                  ALU.subtract, ALU.mult).then_inc(zn_done, 1)

            def sz_lo_part(g):
                dve.wait_ge(sz_hi_done, g.n + 1)
                dve.tensor_tensor(sz_lo[:], A2[:, 0:H], sz_hi[:].bitcast(F32), ALU.subtract)\
                    .then_inc(sz_split, 1)

            def x3_sum(g):
                dve.wait_ge(w2_done, g.n + 1)
                dve.wait_ge(base_done, g.n + 1)
                wait(dve, h3_done, g.n - 1)
                wait(dve, y_done, g.n - 1)
                dve.scalar_tensor_tensor(x3[:, g.s2, :], B2[:, 0:F], d_inv[:, g.s:g.s + 1],
                                         base[:, g.s2, :], ALU.mult, ALU.add).then_inc(x3_done, 1)
                dve.wait_ge(x3_done, g.n + 1)
                norm_stats(3, g, x3[:, g.s2, :], shift_done[3])

            def h3_lo(g):
                dve.wait_ge(h3_hi_done, g.n + 1)
                dve.tensor_tensor(h3t_lo[:], A3[:, 0:F], h3t_hi[:].bitcast(F32), ALU.subtract)\
                    .then_inc(h3_split, 1)

            def gate(g):
                dve.wait_ge(t_copied, g.n + 1)
                dve.wait_ge(agg3_done, g.n + 1)
                dve.tensor_tensor_reduce(prod[:], A3[:, 0:F], t32[:], 1.0, 0.0, ALU.mult, ALU.add,
                                         w_raw[:]).then_inc(w_raw_done, 1)
                dve.wait_ge(w_raw_done, g.n + 1)
                wait(dve, e_col_done, g.n)
                dve.tensor_scalar(w_col[:], w_raw[:], mask_scaled[:, bass.ds(g.n, 1)], None, ALU.mult)\
                    .then_inc(w_done, 1)

            def row_max(g):
                dve.wait_ge(w_spread, g.n + 1)
                dve.tensor_reduce(neg_max[:], A3[:, 0:N], AX.X, ALU.max, negate=True).then_inc(max_done, 1)

            def result(g):
                dve.wait_ge(e_row_done, g.n + 1)
                dve.reciprocal(e_inv[:], e_sum[:]).then_inc(e_inv_done, 1)
                dve.wait_ge(e_inv_done, g.n + 1)
                dve.wait_ge(e_col_done, g.n + 1)
                dve.tensor_tensor(p_col[:], e_col[:], e_inv[:], ALU.mult).then_inc(p_done, 1)
                dve.wait_ge(p_done, g.n + 1)
                if not isinstance(g.n, int):
                    dve.wait_ge(y_stored[g.s2], (g.n - g.s2) * 8)
                elif g.n >= 2:
                    dve.wait_ge(y_stored[g.s2], g.n // 2 * 16)
                dve.scalar_tensor_tensor(y[:, g.s2, :], B3[:, F:2 * F], p_col[:], x3[:, g.s2, :],
                                         ALU.mult, ALU.add).then_inc(y_done, 1)

            def step(t, k):
                if (g := in_flight(t, k, 3, G)):
                    x2_sum(g)
                if (g := in_flight(t, k, 2, G)):
                    h1_lo(g)
                if (g := in_flight(t, k, 1, G)):
                    l0_split_(g)
                if (g := in_flight(t, k, 4, G)):
                    hidden_norm(g)
                if (g := in_flight(t, k, 5, G)):
                    gate(g)
                if (g := in_flight(t, k, 1, G)):
                    edges(g)
                if (g := in_flight(t, k, 2, G)):
                    si_add(g)
                if (g := in_flight(t, k, 0, G)):
                    norm0(g)
                if (g := in_flight(t, k, 4, G)):
                    sz_lo_part(g)
                if (g := in_flight(t, k, 3, G)):
                    sh_lo_part(g)
                if (g := in_flight(t, k, 2, G)):
                    transition(g)
                if (g := in_flight(t, k, 1, G)):
                    node_degrees(g)
                if (g := in_flight(t, k, 5, G)):
                    row_max(g)
                if (g := in_flight(t, k, 4, G)):
                    x3_sum(g)
                if (g := in_flight(t, k, 5, G)):
                    result(g)
                if (g := in_flight(t, k, 1, G)):
                    x1_sum(g)
                if (g := in_flight(t, k, 3, G)):
                    hidden(g)
                if (g := in_flight(t, k, 4, G)):
                    h3_lo(g)

            run_steps(dve, step, G)

        @block.tensor
        def _(pe):
            def group(dst, pairs, start=True, stop=True):
                for i, (a, b) in enumerate(pairs):
                    mm = pe.matmul(dst, a, b, start=start and i == 0, stop=stop and i == len(pairs) - 1,
                                   skip_group_check=not (start and stop))
                return mm

            def split_pairs(a_hi, a_lo, w, c):
                return [(a_hi, w[1][:, c, :]), (a_hi, w[2][:, c, :]), (a_lo, w[1][:, c, :])]

            def by_weight(dst, hi, lo, w, chunks, stop=True):
                pairs = []
                for c in range(chunks):
                    pairs += split_pairs(hi[:, c * P:(c + 1) * P], lo[:, c * P:(c + 1) * P], w, c)
                return group(dst, pairs, stop=stop)

            pe.wait_ge(weights_in, 16 * WEIGHT_LOADS)
            for f in range(FC):
                rows = slice(f * P, (f + 1) * P)
                group(A0[:, f * F:(f + 1) * F],
                      [(wqk_sb[:, d, rows], wqk_sb[:, FC + d, :]) for d in range(FC)])
                group(B0[:, 2 * f:2 * f + 2], [(wv1_sb[:, d, rows], aw_sb[:, d, :]) for d in range(FC)])
            group(A1[:, 0:1], [(bv_sb[:, d:d + 1].to_broadcast([P, P]), aw_sb[:, d, i:i + 1])
                               for d in range(FC) for i in range(2)])
            group(B1[:, 0:F], [(beta_sb[:, c:c + 1].to_broadcast([P, P]), w2_raw[:, c, :])
                               for c in range(HC)]).then_inc(setup_products, 1)
            pe.wait_ge(ident_done, 1)
            pe.wait_ge(consts_done, 1)
            pe.wait_ge(setup_evacuated, 1)
            pe.wait_ge(weights_ready, 2)

            def l0_transposes(g):
                pe.wait_ge(adjn_done, g.n + 1)
                pe.wait_ge(h0_done, g.n + 1)
                loaded(pe, adj_loaded, g)
                wait(pe, sums_copied, g.n)
                pe.transpose(A0[:, 0:N], adj_in[:, g.s, :], ident[:])
                pe.transpose(A0[:, N:2 * N], adj_norm[:, g.s2, :], ident[:])
                for c in range(FC):
                    mm = pe.transpose(A0[:, 2 * N + c * P:2 * N + (c + 1) * P],
                                      h0[:, g.s2, c * P:(c + 1) * P], ident[:])
                mm.then_inc(l0_transposed, 1)

            def l0_gates(g):
                pe.wait_ge(l0_split, g.n + 1)
                wait(pe, x1_done, g.n)
                by_weight(B0[:, :], h0t_hi, h0t_lo, gate0, FC, stop=False).then_inc(gates_done, 1)

            def l0_incidence(g):
                pe.wait_ge(binc_done, g.n + 1)
                inc = inc_t[:, g.s2, :]
                group(A0[:, 0:N], [(inc, binc_hi[:, g.s2, :]), (inc, binc_lo[:, g.s2, :])])
                inc32 = inc.bitcast(F32)
                group(A0[:, N:N + 1], [(inc32, edge_w[:, g.s2, :])])
                group(A0[:, N + 2:N + 3], [(inc32, ones_col[:, 0:1])]).then_inc(s_done, 1)

            def l0_aggregate(g):
                pe.wait_ge(gb_copied, g.n + 1)
                group(B0[:, F:2 * F], [(adjn_t[:, g.s2, :], gb[:])], start=False).then_inc(agg_done, 1)

            def h1_transposes(g):
                pe.wait_ge(h1_done, g.n + 1)
                wait(pe, x2_done, g.n)
                for c in range(FC):
                    mm = pe.transpose(A1[:, c * P:(c + 1) * P], h1[:, c * P:(c + 1) * P], ident[:])
                mm.then_inc(h1_transposed, 1)

            def l1_products(g):
                pe.wait_ge(h1_split, g.n + 1)
                wait(pe, trans_copied, g.n)
                by_weight(B1[:, 0:F + 2], h1t_hi, h1t_lo, k2u, FC).then_inc(g2s_done, 1)
                by_weight(A1[:, :], h1t_hi, h1t_lo, k10, FC, stop=False)
                group(A1[:, F:2 * F], [(spread[:], bias_rows[:])], start=False, stop=False)\
                    .then_inc(g10_done, 1)

            def l1_spread(g):
                pe.wait_ge(g2s_copied, g.n + 1)
                pe.transpose(B1[:, 0:N], g2s[:, F:F + 1].to_broadcast([P, N]), ident[:])\
                    .then_inc(sj_spread, 1)

            def l1_transpose(g):
                pe.wait_ge(trans_done, g.n + 1)
                pe.transpose(B1[:, 0:N], trans[:], ident[:]).then_inc(trans_transposed, 1)

            def l1_hop1(g):
                pe.wait_ge(trans_copied, g.n + 1)
                group(A1[:, 0:F], [(trans_t[:], g2s[:, 0:F])], start=False, stop=False).then_inc(hop1_done, 1)

            def l1_hop2(g):
                pe.wait_ge(q1_done, g.n + 1)
                group(A1[:, F:2 * F], [(trans_t[:], q1[:])], start=False).then_inc(hop2_done, 1)

            def l2_smooth(g):
                pe.wait_ge(h2_done, g.n + 1)
                pe.wait_ge(s_copied, g.n + 1)
                wait(pe, sz_split, g.n)
                for c in range(FC):
                    mm = group(A2[:, c * P:(c + 1) * P], [(h2[:, g.s2, c * P:(c + 1) * P], s_mat[:, g.s, :])])
                mm.then_inc(sh_done, 1)

            def l2_hidden(g):
                pe.wait_ge(sh_split, g.n + 1)
                wait(pe, x3_done, g.n)
                by_weight(B2[:, 0:H], sh_hi, sh_lo, w1, FC).then_inc(w1_done, 1)

            def l2_smooth_hidden(g):
                pe.wait_ge(zn_done, g.n + 1)
                pe.wait_ge(sh_split, g.n + 1)
                for c in range(HC):
                    mm = group(A2[:, c * P:(c + 1) * P], [(zn[:, c * P:(c + 1) * P], s_mat[:, g.s, :])])
                mm.then_inc(sz_done, 1)

            def l2_out(g):
                pe.wait_ge(sz_split, g.n + 1)
                pe.wait_ge(r0_done, g.n + 1)
                by_weight(B2[:, 0:F], sz_hi, sz_lo, w2, HC).then_inc(w2_done, 1)

            def h3_transposes(g):
                pe.wait_ge(h3_done, g.n + 1)
                wait(pe, e_row_done, g.n)
                for c in range(FC):
                    mm = pe.transpose(A3[:, c * P:(c + 1) * P], h3[:, g.s2, c * P:(c + 1) * P], ident[:])
                mm.then_inc(h3_transposed, 1)

            def l3_aggregate(g):
                pe.wait_ge(h3_split, g.n + 1)
                group(A3[:, 0:F], [(adjm_t[:, g.s, :], h3[:, g.s2, :])]).then_inc(agg3_done, 1)

            def l3_products(g):
                wait(pe, y_done, g.n)
                by_weight(B3[:, :], h3t_hi, h3t_lo, mv, FC).then_inc(tv_done, 1)

            def l3_spread(g):
                pe.wait_ge(w_done, g.n + 1)
                pe.transpose(A3[:, 0:N], w_col[:].to_broadcast([P, N]), ident[:]).then_inc(w_spread, 1)

            def step(t, k):
                if (g := in_flight(t, k, 5, G)):
                    l3_aggregate(g)
                if (g := in_flight(t, k, 1, G)):
                    l0_transposes(g)
                if (g := in_flight(t, k, 5, G)):
                    l3_products(g)
                if (g := in_flight(t, k, 2, G)):
                    l1_products(g)
                if (g := in_flight(t, k, 4, G)):
                    l2_smooth_hidden(g)
                if (g := in_flight(t, k, 1, G)):
                    l0_gates(g)
                if (g := in_flight(t, k, 3, G)):
                    l2_smooth(g)
                if (g := in_flight(t, k, 2, G)):
                    l1_spread(g)
                if (g := in_flight(t, k, 4, G)):
                    l2_out(g)
                if (g := in_flight(t, k, 1, G)):
                    l0_incidence(g)
                if (g := in_flight(t, k, 5, G)):
                    l3_spread(g)
                if (g := in_flight(t, k, 2, G)):
                    l1_transpose(g)
                if (g := in_flight(t, k, 1, G)):
                    l0_aggregate(g)
                if (g := in_flight(t, k, 2, G)):
                    l1_hop1(g)
                if (g := in_flight(t, k, 3, G)):
                    l2_hidden(g)
                if (g := in_flight(t, k, 4, G)):
                    h3_transposes(g)
                if (g := in_flight(t, k, 2, G)):
                    l1_hop2(g)
                if (g := in_flight(t, k, 1, G)):
                    h1_transposes(g)

            run_steps(pe, step, G)


def kernel(x, adj, nodemask, L0_gnn_W, L1_gnn_Wv, L1_gnn_bv, L1_gnn_aw, L1_gnn_ab, L1_gnn_Wk, L1_gnn_bk,
           L2_gnn_W1, L2_gnn_b1, L2_gnn_gamma, L2_gnn_beta, L2_gnn_W2, L2_gnn_b2, L3_gnn_Wqk, L3_gnn_Wv):
    import numpy as np
    import concourse.bacc as bacc
    from concourse.bass_utils import run_bass_kernel_spmd

    def columns(v):
        v = np.asarray(v)
        return v.reshape(-1, P).T

    aw = np.asarray(L1_gnn_aw).reshape(2, -1, P).transpose(2, 1, 0)
    arrays = {
        "x": x, "adj": adj, "mask_t": np.asarray(nodemask).T, "w0t": np.asarray(L0_gnn_W).T,
        "wk": L1_gnn_Wk, "w1t": np.asarray(L2_gnn_W1).T, "w2t": np.asarray(L2_gnn_W2).T,
        "wv3": L3_gnn_Wv, "wqk_t": np.asarray(L3_gnn_Wqk).T, "wv1t": np.asarray(L1_gnn_Wv).T,
        "aw": aw, "bv": columns(L1_gnn_bv), "ab": L1_gnn_ab, "bk": L1_gnn_bk, "b1": L2_gnn_b1,
        "b2": L2_gnn_b2, "gamma": columns(L2_gnn_gamma), "beta": columns(L2_gnn_beta),
    }
    arrays = {n: np.ascontiguousarray(a) for n, a in arrays.items()}
    nc = bacc.Bacc("TRN2", target_bir_lowering=False, num_devices=1)
    args = {n: nc.dram_tensor(n, a.shape, mybir.dt.from_np(a.dtype), kind="ExternalInput").ap()
            for n, a in arrays.items()}
    out = nc.dram_tensor("out", arrays["x"].shape, F32, kind="ExternalOutput").ap()
    build(nc, out=out, **args)
    r = run_bass_kernel_spmd(nc, [arrays], core_ids=[0])
    return r.results[0]["out"]
```

```python
from contextlib import ExitStack

import concourse.bass as bass
from concourse import mybir

F32 = mybir.dt.float32
F32R = mybir.dt.float32r
ALU = mybir.AluOpType
ACT = mybir.ActivationFunctionType
AX = mybir.AxisListType

P = 128
SLOTS = 4
EPS = 1e-5
DEPTH = 6

FIRST_LOOP_STEP = 8


class Graph:

    def __init__(self, n, s):
        self.n = n
        self.s = s
        self.s2 = s % 2


def in_flight(t, k, back, graphs):
    if isinstance(t, int) and not 0 <= t - back < graphs:
        return None
    return Graph(t - back, (k - back) % SLOTS)


def wait(eng, sem, count):
    if not isinstance(count, int) or count > 0:
        eng.wait_ge(sem, count)


def constant_wait(eng, sem):
    eng.wait_ge(sem, 1)


def run_steps(eng, step, graphs):
    for t in range(FIRST_LOOP_STEP):
        step(t, t % SLOTS)
    with eng.Fori(FIRST_LOOP_STEP, graphs - SLOTS + 1, SLOTS) as t0:
        for k in range(SLOTS):
            step(t0 + k, k)
    for t in range(graphs, graphs + DEPTH + 1):
        step(t, t % SLOTS)


def build(nc, x, adj, adj_tr, mask_t, w0t, wk, w1t, w2t, wv3, wqk_t, wv1t, aw, bv, ab, bk, b1, b2, gamma, beta, out):
    G, N, F = x.shape
    FC = F // P
    H = w1t.shape[1]
    HC = H // P
    K = bk.shape[0]
    assert N == P and F == 2 * P and H == 2 * F and K == 3 and (G - FIRST_LOOP_STEP) % SLOTS == 0
    SCORE_SCALE = float(F) ** -0.5

    with ExitStack() as ctx:
        def sb(name, shape, dt=F32):
            return ctx.enter_context(nc.sbuf_tensor(name, shape, dt))

        def sem(name):
            return ctx.enter_context(nc.semaphore(name))

        parts = [("gate0", FC * 2 * F), ("k10", FC * 2 * F), ("k2u", FC * (F + 2)),
                 ("w1", FC * H), ("w2", HC * F), ("mv", FC * 2 * F)]
        at, col = {}, 0
        for name, width in parts:
            at[name] = (col, col + width)
            col += width
        w32 = sb("w32", [P, col])
        w_hi = sb("w_hi", [P, col], F32R)
        w_lo = sb("w_lo", [P, col], F32R)

        def weight(tile, name, chunks):
            return tile[:, at[name][0]:at[name][1]].rearrange("p (c n) -> p c n", c=chunks)

        gate0 = [weight(w, "gate0", FC) for w in (w32, w_hi, w_lo)]
        k10 = [weight(w, "k10", FC) for w in (w32, w_hi, w_lo)]
        k2u = [weight(w, "k2u", FC) for w in (w32, w_hi, w_lo)]
        w1 = [weight(w, "w1", FC) for w in (w32, w_hi, w_lo)]
        w2 = [weight(w, "w2", HC) for w in (w32, w_hi, w_lo)]
        mv = [weight(w, "mv", FC) for w in (w32, w_hi, w_lo)]

        w2_raw = sb("w2_raw", [P, HC, F])
        wqk_sb = sb("wqk_sb", [P, 2 * FC, F])
        wv1_sb = sb("wv1_sb", [P, FC, F])
        aw_sb = sb("aw_sb", [P, FC, 2])
        bv_sb = sb("bv_sb", [P, FC])
        gamma_sb = sb("gamma_sb", [P, HC])
        beta_sb = sb("beta_sb", [P, HC])
        ab_sb = sb("ab_sb", [P, 1])
        bk3 = sb("bk3", [P, K, F])
        bk_sum = sb("bk_sum", [P, F])
        bk_hi = sb("bk_hi", [P, F], F32R)
        bias_rows = sb("bias_rows", [P, F], F32R)
        spread32 = sb("spread32", [P, P])
        spread = sb("spread", [P, P], F32R)
        b1_rows = sb("b1_rows", [P, H])
        b2_rows = sb("b2_rows", [P, F])
        beta_w2 = sb("beta_w2", [P, F])
        score_bias = sb("score_bias", [P, 1])
        mask_sb = sb("mask_sb", [P, G])
        mask_scaled = sb("mask_scaled", [P, G])
        ident = sb("ident", [P, P])
        minus_half = sb("minus_half", [P, 1])

        x_in = sb("x_in", [P, SLOTS, F])
        adj_in = sb("adj_in", [P, SLOTS, N])
        adj_t = sb("adj_t", [P, SLOTS, 1 + N])
        stats = {n: sb(f"stats_{n}", [P, 6]) for n in range(5)}
        mean_var = {n: sb(f"mean_var_{n}", [P, 2, 2]) for n in range(5)}
        var_eps = {n: sb(f"var_eps_{n}", [P, 1]) for n in range(5)}
        rstd = {n: sb(f"rstd_{n}", [P, 2]) for n in range(5)}
        shift = {n: sb(f"shift_{n}", [P, 2]) for n in range(5)}
        deg = sb("deg", [P, 1])
        deg_max = sb("deg_max", [P, 1])
        deg_inv = sb("deg_inv", [P, 2])
        adj_norm = sb("adj_norm", [P, 2, N])
        h0 = sb("h0", [P, 2, F])
        adjm_t = sb("adjm_t", [P, SLOTS, N])
        adjn_t = sb("adjn_t", [P, 2, N])
        h0t_hi = sb("h0t_hi", [P, F], F32R)
        h0t_lo = sb("h0t_lo", [P, F], F32R)
        inc_t = sb("inc_t", [P, 2, N], F32R)
        edge_size = sb("edge_size", [P, 1])
        edge_max = sb("edge_max", [P, 1])
        b_inv = sb("b_inv", [P, 1])
        b_hi = sb("b_hi", [P, 1], F32R)
        b_lo = sb("b_lo", [P, 1])
        binc_hi = sb("binc_hi", [P, 2, N], F32R)
        binc_lo = sb("binc_lo", [P, 2, N], F32R)
        gb = sb("gb", [P, F])
        s_mat = sb("s_mat", [P, SLOTS, N])
        node_sum = sb("node_sum", [P, 2])
        d_max = sb("d_max", [P, 1])
        d_rec = sb("d_rec", [P, 1])
        d_inv = sb("d_inv", [P, SLOTS])
        rho = sb("rho", [P, SLOTS])
        x1 = sb("x1", [P, SLOTS, F])
        h1 = sb("h1", [P, F])
        h1t_hi = sb("h1t_hi", [P, F], F32R)
        h1t_lo = sb("h1t_lo", [P, F], F32R)
        g2s = sb("g2s", [P, F + 2])
        si = sb("si", [P, 2])
        z_max = sb("z_max", [P, N])
        z_exp = sb("z_exp", [P, N])
        alpha = sb("alpha", [P, N])
        row_sum = sb("row_sum", [P, 1])
        row_eps = sb("row_eps", [P, 1])
        row_inv = sb("row_inv", [P, 1])
        trans = sb("trans", [P, N])
        trans_t = sb("trans_t", [P, N])
        q1 = sb("q1", [P, F])
        x2 = sb("x2", [P, 2, F])
        x2b = sb("x2b", [P, F])
        h2 = sb("h2", [P, 2, F])
        base_h = sb("base_h", [P, F])
        base_r = sb("base_r", [P, F])
        base = sb("base", [P, 2, F])
        sh_hi = sb("sh_hi", [P, F], F32R)
        sh_lo = sb("sh_lo", [P, F], F32R)
        r0 = sb("r0", [P, H])
        r1 = sb("r1", [P, H])
        zn = sb("zn", [P, H])
        sz_hi = sb("sz_hi", [P, H], F32R)
        sz_lo = sb("sz_lo", [P, H], F32R)
        x3 = sb("x3", [P, 2, F])
        h3 = sb("h3", [P, 2, F])
        h3t_hi = sb("h3t_hi", [P, F], F32R)
        h3t_lo = sb("h3t_lo", [P, F], F32R)
        t32 = sb("t32", [P, F])
        prod = sb("prod", [P, F])
        w_raw = sb("w_raw", [P, 1])
        w_col = sb("w_col", [P, 1])
        neg_max = sb("neg_max", [P, 1])
        e_row = sb("e_row", [P, N])
        e_sum = sb("e_sum", [P, 1])
        e_col = sb("e_col", [P, 1])
        e_inv = sb("e_inv", [P, 1])
        p_col = sb("p_col", [P, 1])
        y = sb("y", [P, 2, F])

        bank = [ctx.enter_context(nc.psum_tensor(f"bank{n}", [P, 512], F32)) for n in range(8)]
        A0, B0, A1, B1, A2, B2, A3, B3 = bank

        (weights_in, ident_zero, ident_done, consts_done, setup_products, setup_evacuated,
         w32_done, w_hi_done, bias_summed, bias_hi_done, weights_ready) = [sem(n) for n in (
             "weights_in", "ident_zero", "ident_done", "consts_done", "setup_products",
             "setup_evacuated", "w32_done", "w_hi_done", "bias_summed", "bias_hi_done",
             "weights_ready")]
        x_loaded = [sem(f"x_loaded{i}") for i in range(SLOTS)]
        adj_loaded = [sem(f"adj_loaded{i}") for i in range(SLOTS)]
        adj_t_loaded = [sem(f"adj_t_loaded{i}") for i in range(SLOTS)]
        y_stored = [sem(f"y_stored{i}") for i in range(2)]
        stats_done = [sem(f"stats_done{i}") for i in range(5)]
        aggr_done = [sem(f"aggr_done{i}") for i in range(5)]
        var_done = [sem(f"var_done{i}") for i in range(5)]
        rstd_done = [sem(f"rstd_done{i}") for i in range(5)]
        shift_done = [sem(f"shift_done{i}") for i in range(5)]
        names = """adjm_done deg_done deg_clamped deg_ready adjn_done h0_done l0_transposed l0_copied inc_done
            binv_clamped binv_done bhi_done blo_done binc_done l0_split gates_done gb_copied
            s_done s_copied sums_copied dclamp_done drec_done dinv_done d_done agg_done x1_done h1_done
            h1_transposed h1_hi_done h1_split g2s_done g10_done g2s_copied si_done sj_spread
            exp_max_done exp_done alpha_done row_eps_done row_inv_done trans_done trans_transposed
            trans_copied hop1_done q1_done hop2_done x2_done h2_done x2b_done base_h_done
            base_r_done base_done sh_done sh_hi_done sh_split w1_done r0_done r1_done zn_done
            sz_done sz_hi_done sz_split w2_done x3_done h3_done h3_transposed h3_hi_done h3_split
            agg3_done tv_done t_copied w_raw_done w_done w_spread max_done e_row_done e_col_done
            e_inv_done p_done y_done""".split()
        S = {n: sem(n) for n in names}
        (adjm_done, deg_done, deg_clamped, deg_ready, adjn_done, h0_done, l0_transposed, l0_copied, inc_done,
         binv_clamped, binv_done, bhi_done, blo_done, binc_done, l0_split, gates_done, gb_copied,
         s_done, s_copied, sums_copied, dclamp_done, drec_done, dinv_done, d_done, agg_done, x1_done, h1_done,
         h1_transposed, h1_hi_done, h1_split, g2s_done, g10_done, g2s_copied, si_done, sj_spread,
         exp_max_done, exp_done, alpha_done, row_eps_done, row_inv_done, trans_done, trans_transposed,
         trans_copied, hop1_done, q1_done, hop2_done, x2_done, h2_done, x2b_done, base_h_done,
         base_r_done, base_done, sh_done, sh_hi_done, sh_split, w1_done, r0_done, r1_done, zn_done,
         sz_done, sz_hi_done, sz_split, w2_done, x3_done, h3_done, h3_transposed, h3_hi_done,
         h3_split, agg3_done, tv_done, t_copied, w_raw_done, w_done, w_spread, max_done, e_row_done,
         e_col_done, e_inv_done, p_done, y_done) = [S[n] for n in names]

        def loaded(eng, sems, g):
            count = ((g.n - g.s) // SLOTS + 1) * 16 if isinstance(g.n, int) else (g.n - g.s) * 4 + 16
            eng.wait_ge(sems[g.s], count)

        block = ctx.enter_context(nc.Block())

        @block.sync
        def _(sp):
            def c(ap, chunks):
                return ap.rearrange("(c p) n -> p c n", c=chunks)

            for dst, src in (
                (gate0[0][:, :, 0:F], c(w0t[F:2 * F, :], FC)), (gate0[0][:, :, F:2 * F], c(w0t[0:F, :], FC)),
                (k10[0][:, :, 0:F], c(wk[1], FC)), (k10[0][:, :, F:2 * F], c(wk[0], FC)),
                (k2u[0][:, :, 0:F], c(wk[2], FC)), (w1[0], c(w1t, FC)), (w2_raw[:], c(w2t, HC)),
                (mv[0][:, :, F:2 * F], c(wv3, FC)), (wqk_sb[:], c(wqk_t, 2 * FC)),
                (wv1_sb[:], c(wv1t, FC)), (aw_sb[:], aw), (bv_sb[:], bv), (gamma_sb[:], gamma),
                (beta_sb[:], beta), (mask_sb[:], mask_t),
                (ab_sb[:], ab.rearrange("(a n) -> a n", a=1).to_broadcast([P, 1])),
                (b1_rows[:], b1.rearrange("(a n) -> a n", a=1).to_broadcast([P, H])),
                (b2_rows[:], b2.rearrange("(a n) -> a n", a=1).to_broadcast([P, F])),
            ):
                sp.dma_start(dst, src).then_inc(weights_in, 16)
            for k in range(K):
                sp.dma_start(bk3[:, k, :], bk[k:k + 1, :].to_broadcast([P, F])).then_inc(weights_in, 16)

            def load(g):
                wait(sp, x1_done, g.n - SLOTS + 1)
                sp.dma_start(x_in[:, g.s, :], x[g.n]).then_inc(x_loaded[g.s], 16)
                wait(sp, s_done, g.n - SLOTS + 1)
                wait(sp, adjm_done, g.n - SLOTS + 1)
                wait(sp, inc_done, g.n - SLOTS + 1)
                sp.dma_start(adj_t[:, g.s, 1:1 + N], adj_tr[g.n]).then_inc(adj_t_loaded[g.s], 16)
                wait(sp, deg_done, g.n - SLOTS + 1)
                wait(sp, adjn_done, g.n - SLOTS + 1)
                wait(sp, alpha_done, g.n - SLOTS + 1)
                sp.dma_start(adj_in[:, g.s, :], adj[g.n]).then_inc(adj_loaded[g.s], 16)

            def store(g):
                wait(sp, y_done, g.n + 1)
                sp.dma_start(out[g.n], y[:, g.s2, :]).then_inc(y_stored[g.s2], 16)

            def step(t, k):
                if (g := in_flight(t, k, 0, G)):
                    load(g)
                if (g := in_flight(t, k, DEPTH + 1, G)):
                    store(g)

            run_steps(sp, step, G)
            for i in range(2):
                sp.wait_ge(y_stored[i], 16 * G // 2)

        WEIGHT_LOADS = 18 + K

        @block.gpsimd
        def _(pool):
            pool.memset(minus_half[:], -0.5)
            pool.memset(adj_t[:, :, 0:1], 1.0)
            pool.memset(spread32[:], 2.0 / P).then_inc(consts_done, 1)
            pool.memset(ident[:], 0.0).then_inc(ident_zero, 1)
            pool.wait_ge(ident_zero, 1)
            pool.affine_select(out=ident[:], in_=ident[:], compare_op=ALU.not_equal, fill=1.0, base=0,
                               pattern=[[-1, P]], channel_multiplier=1).then_inc(ident_done, 1)
            pool.wait_ge(consts_done, 1)
            pool.wait_ge(weights_ready, 1)

            def rstd_of(n, g, used):
                wait(pool, used, g.n - 1)
                pool.wait_ge(var_done[n], g.n + 1)
                r = rstd[n][:, g.s2:g.s2 + 1]
                pool.tensor_tensor(r, var_eps[n][:], minus_half[:], ALU.pow).then_inc(rstd_done[n], 1)

            def shift_of(n, g):
                constant_wait(pool, consts_done)
                pool.wait_ge(rstd_done[n], g.n + 1)
                pool.tensor_scalar(shift[n][:, g.s2:g.s2 + 1], mean_var[n][:, g.s2, 0:1],
                                   rstd[n][:, g.s2:g.s2 + 1], -1.0, ALU.mult, ALU.mult)\
                    .then_inc(shift_done[n], 1)

            norm_used = (h0_done, h1_done, h2_done, h3_done, zn_done)
            rstd0, rstd1, rstd2, rstd3, rstd4 = [lambda g, n=n: rstd_of(n, g, norm_used[n]) for n in range(5)]
            shift0, shift1, shift2, shift3, shift4 = [lambda g, n=n: shift_of(n, g) for n in range(5)]

            def base_x(g):
                pool.wait_ge(x2_done, g.n + 1)
                wait(pool, base_h_done, g.n)
                pool.tensor_tensor(x2b[:], x2[:, g.s2, :], b2_rows[:], ALU.add).then_inc(x2b_done, 1)

            def base_beta(g):
                constant_wait(pool, consts_done)
                pool.wait_ge(d_done, g.n + 1)
                wait(pool, base_done, g.n)
                pool.tensor_scalar(base_r[:], beta_w2[:], rho[:, g.s:g.s + 1], 1.0, ALU.mult, ALU.mult)\
                    .then_inc(base_r_done, 1)

            def base_h2(g):
                pool.wait_ge(h2_done, g.n + 1)
                pool.wait_ge(x2b_done, g.n + 1)
                wait(pool, base_done, g.n)
                pool.tensor_tensor(base_h[:], x2b[:], h2[:, g.s2, :], ALU.add).then_inc(base_h_done, 1)

            def base_sum(g):
                pool.wait_ge(base_h_done, g.n + 1)
                pool.wait_ge(base_r_done, g.n + 1)
                wait(pool, x3_done, g.n - 1)
                pool.tensor_tensor(base[:, g.s2, :], base_h[:], base_r[:], ALU.add).then_inc(base_done, 1)

            def step(t, k):
                for piece, back in ((shift0, 1), (base_x, 4), (rstd1, 2), (base_h2, 4), (shift1, 2),
                    (base_sum, 4), (rstd4, 4), (shift4, 4), (rstd2, 3), (shift2, 3), (base_beta, 3),
                    (rstd0, 0), (rstd3, 5), (shift3, 5)):
                    if (g := in_flight(t, k, back, G)):
                        piece(g)

            run_steps(pool, step, G)

        @block.scalar
        def _(act):
            act.wait_ge(weights_in, 16 * WEIGHT_LOADS)
            act.wait_ge(w32_done, 1)
            act.activation(w_hi[:], w32[:], ACT.Copy).then_inc(w_hi_done, 1)
            act.wait_ge(bias_summed, 2)
            act.activation(bk_hi[:], bk_sum[:], ACT.Copy).then_inc(bias_hi_done, 1)
            act.wait_ge(consts_done, 1)
            act.activation(spread[:], spread32[:], ACT.Copy).then_inc(weights_ready, 1)

            def norm(n, g, dst, src, done, func=ACT.Relu):
                act.wait_ge(shift_done[n], g.n + 1)
                act.activation(dst, src, func, bias=shift[n][:, g.s2:g.s2 + 1],
                               scale=rstd[n][:, g.s2:g.s2 + 1]).then_inc(done, 1)

            def adj_normalised(g):
                loaded(act, adj_loaded, g)
                act.wait_ge(deg_ready, g.n + 1)
                wait(act, l0_transposed, g.n - 1)
                act.activation(adj_norm[:, g.s2, :], adj_in[:, g.s, :], ACT.Copy,
                               scale=deg_inv[:, g.s2:g.s2 + 1]).then_inc(adjn_done, 1)

            def norm0(g):
                loaded(act, x_loaded, g)
                wait(act, l0_transposed, g.n - 1)
                norm(0, g, h0[:, g.s2, :], x_in[:, g.s, :], h0_done)

            def adjm(g):
                loaded(act, adj_t_loaded, g)
                wait(act, agg3_done, g.n - SLOTS + 1)
                act.activation(adjm_t[:, g.s, :], adj_t[:, g.s, 1:1 + N], ACT.Copy,
                               scale=mask_sb[:, bass.ds(g.n, 1)]).then_inc(adjm_done, 1)

            def l0_copies(g):
                act.wait_ge(l0_transposed, g.n + 1)
                wait(act, agg_done, g.n - 1)
                act.activation(adjn_t[:, g.s2, :], A0[:, 0:N], ACT.Copy)
                act.activation(h0t_hi[:], A0[:, N:N + F], ACT.Copy).then_inc(l0_copied, 1)

            def edge_scale(g):
                act.wait_ge(blo_done, g.n + 1)
                act.wait_ge(inc_done, g.n + 1)
                wait(act, s_done, g.n - 1)
                inc32 = inc_t[:, g.s2, :].bitcast(F32)
                act.activation(binc_hi[:, g.s2, :], inc32, ACT.Copy, scale=b_hi[:].bitcast(F32))
                act.activation(binc_lo[:, g.s2, :], inc32, ACT.Copy, scale=b_lo[:]).then_inc(binc_done, 1)

            def gb_copy(g):
                act.wait_ge(gates_done, g.n + 1)
                act.activation(gb[:], B0[:, 0:F], ACT.Copy).then_inc(gb_copied, 1)

            def s_copy(g):
                act.wait_ge(s_done, g.n + 1)
                wait(act, sz_done, g.n - SLOTS + 1)
                wait(act, dclamp_done, g.n)
                wait(act, d_done, g.n)
                act.activation(s_mat[:, g.s, :], A0[:, 0:N], ACT.Copy).then_inc(s_copied, 1)
                act.activation(node_sum[:], A0[:, N:N + 2], ACT.Copy).then_inc(sums_copied, 1)

            def norm1(g):
                wait(act, h1_transposed, g.n)
                norm(1, g, h1[:], x1[:, g.s, :], h1_done)

            def h1_hi(g):
                act.wait_ge(h1_transposed, g.n + 1)
                act.activation(h1t_hi[:], A1[:, 0:F], ACT.Copy).then_inc(h1_hi_done, 1)

            def g2s_copy(g):
                act.wait_ge(g2s_done, g.n + 1)
                act.activation(g2s[:], B1[:, 0:F + 2], ACT.Copy).then_inc(g2s_copied, 1)

            def scores(g):
                act.wait_ge(sj_spread, g.n + 1)
                act.wait_ge(si_done, g.n + 1)
                wait(act, exp_max_done, g.n)
                act.activation(z_exp[:], B1[:, 0:N], ACT.Exp, bias=si[:, 0:1])
                act.activation(B1[:, N:2 * N], B1[:, 0:N], ACT.Exp, bias=si[:, 1:2], scale=0.2)\
                    .then_inc(exp_done, 1)

            def trans_copy(g):
                act.wait_ge(trans_transposed, g.n + 1)
                act.activation(trans_t[:], B1[:, 0:N], ACT.Copy).then_inc(trans_copied, 1)

            def q1_copy(g):
                act.wait_ge(hop1_done, g.n + 1)
                act.activation(q1[:], A1[:, 0:F], ACT.Copy).then_inc(q1_done, 1)

            def norm2(g):
                wait(act, sh_done, g.n - 1)
                wait(act, base_h_done, g.n - 1)
                norm(2, g, h2[:, g.s2, :], x2[:, g.s2, :], h2_done)

            def sh_hi_copy(g):
                act.wait_ge(sh_done, g.n + 1)
                act.activation(sh_hi[:], A2[:, 0:F], ACT.Copy).then_inc(sh_hi_done, 1)

            def hidden_relu(g):
                act.wait_ge(r0_done, g.n + 1)
                wait(act, zn_done, g.n)
                act.activation(r1[:], r0[:], ACT.Relu).then_inc(r1_done, 1)

            def norm4(g):
                wait(act, sz_done, g.n)
                norm(4, g, zn[:], r1[:], zn_done, ACT.Identity)

            def sz_hi_copy(g):
                act.wait_ge(sz_done, g.n + 1)
                act.activation(sz_hi[:], A2[:, 0:H], ACT.Copy).then_inc(sz_hi_done, 1)

            def norm3(g):
                wait(act, agg3_done, g.n - 1)
                norm(3, g, h3[:, g.s2, :], x3[:, g.s2, :], h3_done)

            def h3_hi(g):
                act.wait_ge(h3_transposed, g.n + 1)
                act.activation(h3t_hi[:], A3[:, 0:F], ACT.Copy).then_inc(h3_hi_done, 1)

            def t_copy(g):
                act.wait_ge(tv_done, g.n + 1)
                wait(act, w_raw_done, g.n)
                act.activation(t32[:], B3[:, 0:F], ACT.Copy).then_inc(t_copied, 1)

            def softmax(g):
                act.wait_ge(max_done, g.n + 1)
                wait(act, p_done, g.n)
                act.activation(e_row[:], A3[:, 0:N], ACT.Exp, bias=neg_max[:], accum_out=e_sum[:])\
                    .then_inc(e_row_done, 1)
                act.activation(e_col[:], w_col[:], ACT.Exp, bias=neg_max[:]).then_inc(e_col_done, 1)

            def step(t, k):
                for piece, back in ((h3_hi, 6), (l0_copies, 1), (q1_copy, 3), (norm1, 2),
                    (hidden_relu, 4), (h1_hi, 2), (edge_scale, 1), (t_copy, 6), (gb_copy, 1),
                    (adj_normalised, 0), (norm4, 4), (g2s_copy, 2), (norm2, 3), (sz_hi_copy, 4),
                    (adjm, 3), (scores, 2), (s_copy, 1), (softmax, 6), (sh_hi_copy, 3), (norm0, 0),
                    (norm3, 5), (trans_copy, 2)):
                    if (g := in_flight(t, k, back, G)):
                        piece(g)

            run_steps(act, step, G)

        @block.vector
        def _(dve):
            dve.wait_ge(weights_in, 16 * WEIGHT_LOADS)
            dve.tensor_scalar(mask_scaled[:], mask_sb[:], SCORE_SCALE, None, ALU.mult)
            for c in range(HC):
                dve.tensor_scalar(w2[0][:, c, :], w2_raw[:, c, :], gamma_sb[:, c:c + 1], None, ALU.mult)
            dve.tensor_tensor(bk_sum[:], bk3[:, 0, :], bk3[:, 1, :], ALU.add).then_inc(bias_summed, 1)
            dve.wait_ge(bias_summed, 1)
            dve.tensor_tensor(bk_sum[:], bk_sum[:], bk3[:, 2, :], ALU.add).then_inc(bias_summed, 1)
            dve.wait_ge(setup_products, 1)
            dve.tensor_copy(mv[0][:, :, 0:F], A0[:].rearrange("p (c n) -> p c n", c=FC))
            dve.tensor_copy(k2u[0][:, :, F:F + 2], B0[:, 0:2 * FC].rearrange("p (c n) -> p c n", c=FC))\
                .then_inc(w32_done, 1)
            dve.tensor_tensor(score_bias[:], A1[:, 0:1], ab_sb[:], ALU.add)
            dve.tensor_copy(beta_w2[:], B1[:, 0:F]).then_inc(setup_evacuated, 1)
            dve.wait_ge(w_hi_done, 1)
            dve.tensor_tensor(w_lo[:], w32[:], w_hi[:].bitcast(F32), ALU.subtract)
            dve.wait_ge(bias_hi_done, 1)
            dve.tensor_copy(bias_rows[0:P // 2, :], bk_hi[0:P // 2, :].bitcast(F32))
            dve.tensor_tensor(bias_rows[P // 2:P, :], bk_sum[P // 2:P, :], bk_hi[P // 2:P, :].bitcast(F32),
                              ALU.subtract).then_inc(weights_ready, 1)
            dve.wait_ge(setup_evacuated, 1)

            def norm_stats(n, g, src, src_done):
                if src_done is None:
                    loaded(dve, x_loaded, g)
                else:
                    dve.wait_ge(src_done, g.n + 1)
                wait(dve, aggr_done[n], g.n)
                wait(dve, shift_done[n], g.n - 1)
                dve.bn_stats(stats[n][:], src).then_inc(stats_done[n], 1)

            def norm_mean(n, g):
                constant_wait(dve, weights_ready)
                dve.wait_ge(stats_done[n], g.n + 1)
                dve.bn_aggr(mean_var[n][:, g.s2, :], stats[n][:]).then_inc(aggr_done[n], 1)

            def norm_eps(n, g):
                dve.wait_ge(aggr_done[n], g.n + 1)
                wait(dve, rstd_done[n], g.n)
                dve.tensor_scalar(var_eps[n][:], mean_var[n][:, g.s2, 1:2], EPS, None, ALU.add)\
                    .then_inc(var_done[n], 1)

            def stats0(g):
                dve.wait_ge(deg_done, g.n + 1)
                norm_stats(0, g, x_in[:, g.s, :], None)

            def stats1(g):
                norm_stats(1, g, x1[:, g.s, :], x1_done)

            def stats2(g):
                norm_stats(2, g, x2[:, g.s2, :], x2_done)

            def stats3(g):
                norm_stats(3, g, x3[:, g.s2, :], x3_done)

            def stats4(g):
                norm_stats(4, g, r1[:], r1_done)

            mean0, mean1, mean2, mean3, mean4 = [lambda g, n=n: norm_mean(n, g) for n in range(5)]
            eps0, eps1, eps2, eps3, eps4 = [lambda g, n=n: norm_eps(n, g) for n in range(5)]

            def degree(g):
                loaded(dve, adj_loaded, g)
                wait(dve, deg_clamped, g.n)
                dve.tensor_reduce(deg[:], adj_in[:, g.s, :], AX.X, ALU.add).then_inc(deg_done, 1)

            def degree_clamp(g):
                dve.wait_ge(deg_done, g.n + 1)
                wait(dve, deg_ready, g.n)
                dve.tensor_scalar(deg_max[:], deg[:], 1e-6, None, ALU.max).then_inc(deg_clamped, 1)

            def degree_inv(g):
                dve.wait_ge(deg_clamped, g.n + 1)
                wait(dve, adjn_done, g.n - 1)
                dve.reciprocal(deg_inv[:, g.s2:g.s2 + 1], deg_max[:]).then_inc(deg_ready, 1)

            def h0_lo(g):
                dve.wait_ge(l0_copied, g.n + 1)
                dve.tensor_tensor(h0t_lo[:], A0[:, N:N + F], h0t_hi[:].bitcast(F32), ALU.subtract)\
                    .then_inc(l0_split, 1)

            def incidence(g):
                loaded(dve, adj_t_loaded, g)
                wait(dve, s_done, g.n - 1)
                wait(dve, binv_clamped, g.n)
                dve.tensor_scalar(inc_t[:, g.s2, :], adj_t[:, g.s, 1:1 + N], 0.0, None, ALU.not_equal, ALU.add,
                                  accum_out=edge_size[:]).then_inc(inc_done, 1)

            def edge_clamp(g):
                dve.wait_ge(inc_done, g.n + 1)
                wait(dve, binv_done, g.n)
                dve.tensor_scalar(edge_max[:], edge_size[:], 1.0, None, ALU.max).then_inc(binv_clamped, 1)

            def edge_inv(g):
                dve.wait_ge(binv_clamped, g.n + 1)
                wait(dve, blo_done, g.n)
                dve.reciprocal(b_inv[:], edge_max[:]).then_inc(binv_done, 1)

            def edge_hi(g):
                dve.wait_ge(binv_done, g.n + 1)
                wait(dve, binc_done, g.n)
                dve.tensor_copy(b_hi[:], b_inv[:]).then_inc(bhi_done, 1)

            def edge_lo(g):
                dve.wait_ge(bhi_done, g.n + 1)
                wait(dve, binc_done, g.n)
                dve.tensor_tensor(b_lo[:], b_inv[:], b_hi[:].bitcast(F32), ALU.subtract)\
                    .then_inc(blo_done, 1)

            def node_clamp(g):
                dve.wait_ge(sums_copied, g.n + 1)
                wait(dve, drec_done, g.n)
                dve.tensor_scalar(d_max[:], node_sum[:, 1:2], 1.1754944e-38, None, ALU.max)\
                    .then_inc(dclamp_done, 1)

            def node_rec(g):
                dve.wait_ge(dclamp_done, g.n + 1)
                wait(dve, dinv_done, g.n)
                dve.reciprocal(d_rec[:], d_max[:]).then_inc(drec_done, 1)

            def node_inv(g):
                dve.wait_ge(drec_done, g.n + 1)
                wait(dve, x3_done, g.n - SLOTS + 1)
                dve.scalar_tensor_tensor(d_inv[:, g.s:g.s + 1], node_sum[:, 1:2], 0.0, d_rec[:],
                                         ALU.is_gt, ALU.mult).then_inc(dinv_done, 1)

            def node_rho(g):
                dve.wait_ge(dinv_done, g.n + 1)
                wait(dve, base_r_done, g.n - SLOTS + 1)
                dve.tensor_tensor(rho[:, g.s:g.s + 1], node_sum[:, 0:1], d_inv[:, g.s:g.s + 1], ALU.mult)\
                    .then_inc(d_done, 1)

            def x1_sum(g):
                dve.wait_ge(agg_done, g.n + 1)
                wait(dve, x2_done, g.n - SLOTS + 1)
                loaded(dve, x_loaded, g)
                dve.scalar_tensor_tensor(x1[:, g.s, :], B0[:, F:2 * F], 0.0, x_in[:, g.s, :],
                                         ALU.max, ALU.add).then_inc(x1_done, 1)

            def h1_lo(g):
                dve.wait_ge(h1_hi_done, g.n + 1)
                dve.tensor_tensor(h1t_lo[:], A1[:, 0:F], h1t_hi[:].bitcast(F32), ALU.subtract)\
                    .then_inc(h1_split, 1)

            def si_add(g):
                dve.wait_ge(g2s_copied, g.n + 1)
                wait(dve, exp_done, g.n)
                dve.tensor_scalar(si[:, 0:1], g2s[:, F + 1:F + 2], score_bias[:], None, ALU.add)
                dve.tensor_scalar(si[:, 1:2], g2s[:, F + 1:F + 2], score_bias[:], 0.2, ALU.add, ALU.mult)\
                    .then_inc(si_done, 1)

            def exp_max(g):
                dve.wait_ge(exp_done, g.n + 1)
                wait(dve, alpha_done, g.n)
                dve.tensor_tensor(z_max[:], B1[:, N:2 * N], z_exp[:], ALU.max).then_inc(exp_max_done, 1)

            def attention(g):
                dve.wait_ge(exp_max_done, g.n + 1)
                wait(dve, trans_done, g.n)
                wait(dve, row_eps_done, g.n)
                dve.tensor_tensor_reduce(alpha[:], z_max[:], adj_in[:, g.s, :], 1.0, 0.0, ALU.mult,
                                         ALU.add, row_sum[:]).then_inc(alpha_done, 1)

            def attention_eps(g):
                dve.wait_ge(alpha_done, g.n + 1)
                wait(dve, row_inv_done, g.n)
                dve.tensor_scalar(row_eps[:], row_sum[:], 1e-12, None, ALU.add).then_inc(row_eps_done, 1)

            def attention_inv(g):
                dve.wait_ge(row_eps_done, g.n + 1)
                wait(dve, trans_done, g.n)
                dve.reciprocal(row_inv[:], row_eps[:]).then_inc(row_inv_done, 1)

            def transition(g):
                dve.wait_ge(row_inv_done, g.n + 1)
                wait(dve, trans_transposed, g.n)
                dve.tensor_scalar(trans[:], alpha[:], row_inv[:], None, ALU.mult).then_inc(trans_done, 1)

            def x2_sum(g):
                dve.wait_ge(hop2_done, g.n + 1)
                wait(dve, h2_done, g.n - 1)
                wait(dve, x2b_done, g.n - 1)
                dve.scalar_tensor_tensor(x2[:, g.s2, :], A1[:, F:2 * F], 0.0, x1[:, g.s, :],
                                         ALU.max, ALU.add).then_inc(x2_done, 1)

            def sh_lo_part(g):
                dve.wait_ge(sh_hi_done, g.n + 1)
                dve.tensor_tensor(sh_lo[:], A2[:, 0:F], sh_hi[:].bitcast(F32), ALU.subtract)\
                    .then_inc(sh_split, 1)

            def hidden(g):
                dve.wait_ge(w1_done, g.n + 1)
                wait(dve, r1_done, g.n)
                dve.scalar_tensor_tensor(r0[:], B2[:, 0:H], d_inv[:, g.s:g.s + 1], b1_rows[:],
                                         ALU.mult, ALU.add).then_inc(r0_done, 1)

            def sz_lo_part(g):
                dve.wait_ge(sz_hi_done, g.n + 1)
                dve.tensor_tensor(sz_lo[:], A2[:, 0:H], sz_hi[:].bitcast(F32), ALU.subtract)\
                    .then_inc(sz_split, 1)

            def x3_sum(g):
                dve.wait_ge(w2_done, g.n + 1)
                dve.wait_ge(base_done, g.n + 1)
                wait(dve, h3_done, g.n - 1)
                wait(dve, y_done, g.n - 1)
                dve.scalar_tensor_tensor(x3[:, g.s2, :], B2[:, 0:F], d_inv[:, g.s:g.s + 1],
                                         base[:, g.s2, :], ALU.mult, ALU.add).then_inc(x3_done, 1)

            def h3_lo(g):
                dve.wait_ge(h3_hi_done, g.n + 1)
                dve.tensor_tensor(h3t_lo[:], A3[:, 0:F], h3t_hi[:].bitcast(F32), ALU.subtract)\
                    .then_inc(h3_split, 1)

            def gate(g):
                dve.wait_ge(t_copied, g.n + 1)
                dve.wait_ge(agg3_done, g.n + 1)
                wait(dve, w_done, g.n)
                dve.tensor_tensor_reduce(prod[:], A3[:, 0:F], t32[:], 1.0, 0.0, ALU.mult, ALU.add,
                                         w_raw[:]).then_inc(w_raw_done, 1)

            def gate_scale(g):
                dve.wait_ge(w_raw_done, g.n + 1)
                wait(dve, e_col_done, g.n)
                wait(dve, w_spread, g.n)
                dve.tensor_scalar(w_col[:], w_raw[:], mask_scaled[:, bass.ds(g.n, 1)], None, ALU.mult)\
                    .then_inc(w_done, 1)

            def row_max(g):
                dve.wait_ge(w_spread, g.n + 1)
                dve.tensor_reduce(neg_max[:], A3[:, 0:N], AX.X, ALU.max, negate=True).then_inc(max_done, 1)

            def softmax_inv(g):
                dve.wait_ge(e_row_done, g.n + 1)
                wait(dve, p_done, g.n)
                dve.reciprocal(e_inv[:], e_sum[:]).then_inc(e_inv_done, 1)

            def softmax_p(g):
                dve.wait_ge(e_inv_done, g.n + 1)
                dve.wait_ge(e_col_done, g.n + 1)
                wait(dve, y_done, g.n)
                dve.tensor_tensor(p_col[:], e_col[:], e_inv[:], ALU.mult).then_inc(p_done, 1)

            def result(g):
                dve.wait_ge(p_done, g.n + 1)
                if not isinstance(g.n, int):
                    dve.wait_ge(y_stored[g.s2], (g.n - g.s2) * 8)
                elif g.n >= 2:
                    dve.wait_ge(y_stored[g.s2], g.n // 2 * 16)
                dve.scalar_tensor_tensor(y[:, g.s2, :], B3[:, F:2 * F], p_col[:], x3[:, g.s2, :],
                                         ALU.mult, ALU.add).then_inc(y_done, 1)

            def step(t, k):
                for piece, back in ((incidence, 0), (degree, 0), (edge_clamp, 0), (node_rec, 2),
                    (h3_lo, 6), (degree_clamp, 0), (h0_lo, 1), (stats3, 5), (hidden, 4), (x2_sum, 3),
                    (mean3, 5), (stats0, 0), (stats4, 4), (edge_inv, 0), (node_inv, 2), (mean4, 4),
                    (degree_inv, 0), (eps4, 4), (eps3, 5), (stats2, 3), (h1_lo, 2), (mean0, 0),
                    (mean2, 3), (edge_hi, 0), (eps2, 3), (gate, 6), (gate_scale, 6), (eps0, 0),
                    (x1_sum, 1), (node_rho, 2), (si_add, 2), (stats1, 1), (row_max, 6), (sz_lo_part, 4),
                    (exp_max, 2), (mean1, 1), (edge_lo, 0), (attention, 2), (attention_eps, 2),
                    (attention_inv, 2), (softmax_inv, 6), (node_clamp, 1), (transition, 2), (eps1, 1),
                    (softmax_p, 6), (sh_lo_part, 3), (result, 6), (x3_sum, 4)):
                    if (g := in_flight(t, k, back, G)):
                        piece(g)

            run_steps(dve, step, G)

        @block.tensor
        def _(pe):
            def group(dst, pairs, start=True, stop=True):
                for i, (a, b) in enumerate(pairs):
                    mm = pe.matmul(dst, a, b, start=start and i == 0, stop=stop and i == len(pairs) - 1,
                                   skip_group_check=not (start and stop))
                return mm

            def split_pairs(a_hi, a_lo, w, c):
                return [(a_hi, w[1][:, c, :]), (a_hi, w[2][:, c, :]), (a_lo, w[1][:, c, :])]

            def by_weight(dst, hi, lo, w, chunks, stop=True):
                pairs = []
                for c in range(chunks):
                    pairs += split_pairs(hi[:, c * P:(c + 1) * P], lo[:, c * P:(c + 1) * P], w, c)
                return group(dst, pairs, stop=stop)

            pe.wait_ge(weights_in, 16 * WEIGHT_LOADS)
            for f in range(FC):
                rows = slice(f * P, (f + 1) * P)
                group(A0[:, f * F:(f + 1) * F],
                      [(wqk_sb[:, d, rows], wqk_sb[:, FC + d, :]) for d in range(FC)])
                group(B0[:, 2 * f:2 * f + 2], [(wv1_sb[:, d, rows], aw_sb[:, d, :]) for d in range(FC)])
            group(A1[:, 0:1], [(bv_sb[:, d:d + 1].to_broadcast([P, P]), aw_sb[:, d, i:i + 1])
                               for d in range(FC) for i in range(2)])
            group(B1[:, 0:F], [(beta_sb[:, c:c + 1].to_broadcast([P, P]), w2_raw[:, c, :])
                               for c in range(HC)]).then_inc(setup_products, 1)
            pe.wait_ge(ident_done, 1)
            pe.wait_ge(consts_done, 1)
            pe.wait_ge(setup_evacuated, 1)
            pe.wait_ge(weights_ready, 2)

            def l0_transposes(g):
                pe.wait_ge(adjn_done, g.n + 1)
                pe.wait_ge(h0_done, g.n + 1)
                wait(pe, sums_copied, g.n)
                pe.transpose(A0[:, 0:N], adj_norm[:, g.s2, :], ident[:])
                for c in range(FC):
                    mm = pe.transpose(A0[:, N + c * P:N + (c + 1) * P],
                                      h0[:, g.s2, c * P:(c + 1) * P], ident[:])
                mm.then_inc(l0_transposed, 1)

            def l0_gates(g):
                pe.wait_ge(l0_split, g.n + 1)
                wait(pe, x1_done, g.n)
                by_weight(B0[:, :], h0t_hi, h0t_lo, gate0, FC, stop=False).then_inc(gates_done, 1)

            def l0_incidence(g):
                pe.wait_ge(binc_done, g.n + 1)
                pe.wait_ge(l0_split, g.n + 1)
                loaded(pe, adj_t_loaded, g)
                inc = inc_t[:, g.s2, :]
                group(A0[:, 0:N], [(inc, binc_hi[:, g.s2, :]), (inc, binc_lo[:, g.s2, :])])
                inc32 = inc.bitcast(F32)
                group(A0[:, N:N + 2], [(inc32, adj_t[:, g.s, 0:2])]).then_inc(s_done, 1)

            def l0_aggregate(g):
                pe.wait_ge(gb_copied, g.n + 1)
                group(B0[:, F:2 * F], [(adjn_t[:, g.s2, :], gb[:])], start=False).then_inc(agg_done, 1)

            def h1_transposes(g):
                pe.wait_ge(h1_done, g.n + 1)
                wait(pe, x2_done, g.n)
                for c in range(FC):
                    mm = pe.transpose(A1[:, c * P:(c + 1) * P], h1[:, c * P:(c + 1) * P], ident[:])
                mm.then_inc(h1_transposed, 1)

            def l1_product2(g):
                pe.wait_ge(h1_split, g.n + 1)
                wait(pe, trans_copied, g.n)
                by_weight(B1[:, 0:F + 2], h1t_hi, h1t_lo, k2u, FC).then_inc(g2s_done, 1)

            def l1_products10(g):
                pe.wait_ge(h1_split, g.n + 1)
                by_weight(A1[:, :], h1t_hi, h1t_lo, k10, FC, stop=False)
                group(A1[:, F:2 * F], [(spread[:], bias_rows[:])], start=False, stop=False)\
                    .then_inc(g10_done, 1)

            def l1_spread(g):
                pe.wait_ge(g2s_copied, g.n + 1)
                pe.transpose(B1[:, 0:N], g2s[:, F:F + 1].to_broadcast([P, N]), ident[:])\
                    .then_inc(sj_spread, 1)

            def l1_transpose(g):
                pe.wait_ge(trans_done, g.n + 1)
                pe.transpose(B1[:, 0:N], trans[:], ident[:]).then_inc(trans_transposed, 1)

            def l1_hop1(g):
                pe.wait_ge(trans_copied, g.n + 1)
                group(A1[:, 0:F], [(trans_t[:], g2s[:, 0:F])], start=False, stop=False).then_inc(hop1_done, 1)

            def l1_hop2(g):
                pe.wait_ge(q1_done, g.n + 1)
                group(A1[:, F:2 * F], [(trans_t[:], q1[:])], start=False).then_inc(hop2_done, 1)

            def l2_smooth(g):
                pe.wait_ge(h2_done, g.n + 1)
                pe.wait_ge(s_copied, g.n + 1)
                wait(pe, sz_split, g.n)
                for c in range(FC):
                    mm = group(A2[:, c * P:(c + 1) * P], [(h2[:, g.s2, c * P:(c + 1) * P], s_mat[:, g.s, :])])
                mm.then_inc(sh_done, 1)

            def l2_hidden(g):
                pe.wait_ge(sh_split, g.n + 1)
                wait(pe, x3_done, g.n)
                by_weight(B2[:, 0:H], sh_hi, sh_lo, w1, FC).then_inc(w1_done, 1)

            def l2_smooth_hidden(g):
                pe.wait_ge(zn_done, g.n + 1)
                pe.wait_ge(sh_split, g.n + 1)
                for c in range(HC):
                    mm = group(A2[:, c * P:(c + 1) * P], [(zn[:, c * P:(c + 1) * P], s_mat[:, g.s, :])])
                mm.then_inc(sz_done, 1)

            def l2_out(g):
                pe.wait_ge(sz_split, g.n + 1)
                pe.wait_ge(r0_done, g.n + 1)
                by_weight(B2[:, 0:F], sz_hi, sz_lo, w2, HC).then_inc(w2_done, 1)

            def h3_transposes(g):
                pe.wait_ge(h3_done, g.n + 1)
                wait(pe, e_row_done, g.n)
                for c in range(FC):
                    mm = pe.transpose(A3[:, c * P:(c + 1) * P], h3[:, g.s2, c * P:(c + 1) * P], ident[:])
                mm.then_inc(h3_transposed, 1)

            def l3_aggregate(g):
                pe.wait_ge(h3_split, g.n + 1)
                group(A3[:, 0:F], [(adjm_t[:, g.s, :], h3[:, g.s2, :])]).then_inc(agg3_done, 1)

            def l3_products(g):
                pe.wait_ge(h3_split, g.n + 1)
                wait(pe, y_done, g.n)
                by_weight(B3[:, :], h3t_hi, h3t_lo, mv, FC).then_inc(tv_done, 1)

            def l3_spread(g):
                pe.wait_ge(w_done, g.n + 1)
                pe.transpose(A3[:, 0:N], w_col[:].to_broadcast([P, N]), ident[:]).then_inc(w_spread, 1)

            def step(t, k):
                for piece, back in ((l1_hop2, 3), (l3_products, 6), (h1_transposes, 2), (l0_gates, 1),
                    (l0_incidence, 1), (l3_aggregate, 6), (l1_product2, 2), (l0_aggregate, 1),
                    (l2_smooth_hidden, 4), (l1_spread, 2), (l3_spread, 6), (l1_products10, 2),
                    (l2_smooth, 3), (l2_out, 4), (l1_transpose, 2), (l0_transposes, 0),
                    (h3_transposes, 5), (l1_hop1, 2), (l2_hidden, 3)):
                    if (g := in_flight(t, k, back, G)):
                        piece(g)

            run_steps(pe, step, G)


def kernel(x, adj, nodemask, L0_gnn_W, L1_gnn_Wv, L1_gnn_bv, L1_gnn_aw, L1_gnn_ab, L1_gnn_Wk, L1_gnn_bk,
           L2_gnn_W1, L2_gnn_b1, L2_gnn_gamma, L2_gnn_beta, L2_gnn_W2, L2_gnn_b2, L3_gnn_Wqk, L3_gnn_Wv):
    import numpy as np
    import concourse.bacc as bacc
    from concourse.bass_utils import run_bass_kernel_spmd

    def columns(v):
        v = np.asarray(v)
        return v.reshape(-1, P).T

    aw = np.asarray(L1_gnn_aw).reshape(2, -1, P).transpose(2, 1, 0)
    arrays = {
        "x": x, "adj": adj, "adj_tr": np.asarray(adj).transpose(0, 2, 1), "mask_t": np.asarray(nodemask).T, "w0t": np.asarray(L0_gnn_W).T,
        "wk": L1_gnn_Wk, "w1t": np.asarray(L2_gnn_W1).T, "w2t": np.asarray(L2_gnn_W2).T,
        "wv3": L3_gnn_Wv, "wqk_t": np.asarray(L3_gnn_Wqk).T, "wv1t": np.asarray(L1_gnn_Wv).T,
        "aw": aw, "bv": columns(L1_gnn_bv), "ab": L1_gnn_ab, "bk": L1_gnn_bk, "b1": L2_gnn_b1,
        "b2": L2_gnn_b2, "gamma": columns(L2_gnn_gamma), "beta": columns(L2_gnn_beta),
    }
    arrays = {n: np.ascontiguousarray(a) for n, a in arrays.items()}
    nc = bacc.Bacc("TRN2", target_bir_lowering=False, num_devices=1)
    args = {n: nc.dram_tensor(n, a.shape, mybir.dt.from_np(a.dtype), kind="ExternalInput").ap()
            for n, a in arrays.items()}
    out = nc.dram_tensor("out", arrays["x"].shape, F32, kind="ExternalOutput").ap()
    build(nc, out=out, **args)
    r = run_bass_kernel_spmd(nc, [arrays], core_ids=[0])
    return r.results[0]["out"]
```

```python
from contextlib import ExitStack

import concourse.bass as bass
from concourse import mybir

F32 = mybir.dt.float32
F32R = mybir.dt.float32r
ALU = mybir.AluOpType
ACT = mybir.ActivationFunctionType
AX = mybir.AxisListType

P = 128
SLOTS = 4
LOOP_STEPS = 8
EPS = 1e-5
DEPTH = 6

FIRST_LOOP_STEP = 8


class Graph:

    def __init__(self, n, s):
        self.n = n
        self.s = s
        self.s2 = s % 2


def in_flight(t, k, back, graphs):
    if isinstance(t, int) and not 0 <= t - back < graphs:
        return None
    return Graph(t - back, (k - back) % SLOTS)


def wait(eng, sem, count):
    if not isinstance(count, int) or count > 0:
        eng.wait_ge(sem, count)


def first_use(eng, g, sem, count):
    if isinstance(g.n, int) and g.n == 0:
        eng.wait_ge(sem, count)


def constant_wait(eng, sem):
    eng.wait_ge(sem, 1)


def run_steps(eng, step, graphs, setup=()):
    for t in range(FIRST_LOOP_STEP):
        if t < len(setup):
            setup[t]()
        step(t, t % SLOTS)
    with eng.Fori(FIRST_LOOP_STEP, graphs - LOOP_STEPS + 1, LOOP_STEPS) as t0:
        for k in range(LOOP_STEPS):
            step(t0 + k, k % SLOTS)
    for t in range(graphs, graphs + DEPTH + 1):
        step(t, t % SLOTS)


def build(nc, x, adj, adj_tr, mask_t, w0t, wk, w1t, w2t, wv3, wqk_t, wv1t, aw, bv, ab, bk, b1, b2,
          gamma, beta, out):
    G, N, F = x.shape
    FC = F // P
    H = w1t.shape[1]
    HC = H // P
    K = bk.shape[0]
    assert N == P and F == 2 * P and H == 2 * F and K == 3 and (G - FIRST_LOOP_STEP) % LOOP_STEPS == 0
    SCORE_SCALE = float(F) ** -0.5

    with ExitStack() as ctx:
        def sb(name, shape, dt=F32):
            return ctx.enter_context(nc.sbuf_tensor(name, shape, dt))

        def sem(name):
            return ctx.enter_context(nc.semaphore(name))

        parts = [("gate0", FC * 2 * F), ("k10", FC * 2 * F), ("k2u", FC * (F + 2)),
                 ("w1", FC * H), ("w2", HC * F), ("mv", FC * 2 * F)]
        at, col = {}, 0
        for name, width in parts:
            at[name] = (col, col + width)
            col += width
        w32 = sb("w32", [P, col])
        w_hi = sb("w_hi", [P, col], F32R)
        w_lo = sb("w_lo", [P, col], F32R)

        def weight(tile, name, chunks):
            return tile[:, at[name][0]:at[name][1]].rearrange("p (c n) -> p c n", c=chunks)

        gate0 = [weight(w, "gate0", FC) for w in (w32, w_hi, w_lo)]
        k10 = [weight(w, "k10", FC) for w in (w32, w_hi, w_lo)]
        k2u = [weight(w, "k2u", FC) for w in (w32, w_hi, w_lo)]
        w1 = [weight(w, "w1", FC) for w in (w32, w_hi, w_lo)]
        w2 = [weight(w, "w2", HC) for w in (w32, w_hi, w_lo)]
        mv = [weight(w, "mv", FC) for w in (w32, w_hi, w_lo)]

        w2_raw = sb("w2_raw", [P, HC, F])
        wqk_sb = sb("wqk_sb", [P, 2 * FC, F])
        wv1_sb = sb("wv1_sb", [P, FC, F])
        aw_sb = sb("aw_sb", [P, FC, 2])
        bv_sb = sb("bv_sb", [P, FC])
        gamma_sb = sb("gamma_sb", [P, HC])
        beta_sb = sb("beta_sb", [P, HC])
        ab_sb = sb("ab_sb", [P, 1])
        bk3 = sb("bk3", [P, K, F])
        bk_sum = sb("bk_sum", [P, F])
        bk_hi = sb("bk_hi", [P, F], F32R)
        bias_rows = sb("bias_rows", [P, F], F32R)
        spread32 = sb("spread32", [P, P])
        spread = sb("spread", [P, P], F32R)
        b1_rows = sb("b1_rows", [P, H])
        b2_rows = sb("b2_rows", [P, F])
        beta_w2 = sb("beta_w2", [P, F])
        score_bias = sb("score_bias", [P, 1])
        mask_sb = sb("mask_sb", [P, G])
        mask_scaled = sb("mask_scaled", [P, G])
        ident = sb("ident", [P, P])
        minus_half = sb("minus_half", [P, 1])

        x_in = sb("x_in", [P, SLOTS, F])
        adj_in = sb("adj_in", [P, SLOTS, N])
        adj_t = sb("adj_t", [P, SLOTS, 1 + N])
        stats = {n: sb(f"stats_{n}", [P, 6]) for n in range(5)}
        mean_var = {n: sb(f"mean_var_{n}", [P, SLOTS, 2]) for n in range(5)}
        var_eps = {n: sb(f"var_eps_{n}", [P, SLOTS]) for n in range(5)}
        rstd = {n: sb(f"rstd_{n}", [P, SLOTS]) for n in range(5)}
        shift = {n: sb(f"shift_{n}", [P, SLOTS]) for n in range(5)}
        deg = sb("deg", [P, 2])
        deg_max = sb("deg_max", [P, 2])
        deg_inv = sb("deg_inv", [P, 2])
        adj_norm = sb("adj_norm", [P, 2, N])
        h0 = sb("h0", [P, 2, F])
        adjm_t = sb("adjm_t", [P, SLOTS, N])
        adjn_t = sb("adjn_t", [P, 2, N])
        h0t_hi = sb("h0t_hi", [P, F], F32R)
        h0t_lo = sb("h0t_lo", [P, F], F32R)
        inc_t = sb("inc_t", [P, 2, N], F32R)
        edge_size = sb("edge_size", [P, 2])
        edge_max = sb("edge_max", [P, 2])
        edge_hi = sb("edge_hi", [P, 2, 3 + N], F32R)
        edge_lo = sb("edge_lo", [P, 2, 3 + N], F32R)
        ones_zeros = sb("ones_zeros", [P, 2])
        gb = sb("gb", [P, F])
        s_sums = sb("s_sums", [P, SLOTS, 2 + N])
        d_max = sb("d_max", [P, 2])
        d_rec = sb("d_rec", [P, 2])
        d_inv = sb("d_inv", [P, SLOTS])
        rho = sb("rho", [P, SLOTS])
        x1 = sb("x1", [P, SLOTS, F])
        h1 = sb("h1", [P, F])
        h1t_hi = sb("h1t_hi", [P, F], F32R)
        h1t_lo = sb("h1t_lo", [P, F], F32R)
        g2s = sb("g2s", [P, F + 2])
        si = sb("si", [P, 2])
        z_max = sb("z_max", [P, N])
        z_exp = sb("z_exp", [P, N])
        alpha = sb("alpha", [P, N])
        row_sum = sb("row_sum", [P, 1])
        row_eps = sb("row_eps", [P, 1])
        row_inv = sb("row_inv", [P, 1])
        trans = sb("trans", [P, N])
        trans_t = sb("trans_t", [P, N])
        q1 = sb("q1", [P, F])
        x2 = sb("x2", [P, SLOTS, F])
        x2b = sb("x2b", [P, 2, F])
        h2 = sb("h2", [P, SLOTS, F])
        base_h = sb("base_h", [P, 2, F])
        base_r = sb("base_r", [P, 2, F])
        base = sb("base", [P, SLOTS, F])
        sh_hi = sb("sh_hi", [P, F], F32R)
        sh_lo = sb("sh_lo", [P, F], F32R)
        r0 = sb("r0", [P, H])
        r1 = sb("r1", [P, H])
        zn = sb("zn", [P, H])
        sz_hi = sb("sz_hi", [P, H], F32R)
        sz_lo = sb("sz_lo", [P, H], F32R)
        x3 = sb("x3", [P, SLOTS, F])
        h3 = sb("h3", [P, 2, F])
        h3t_hi = sb("h3t_hi", [P, F], F32R)
        h3t_lo = sb("h3t_lo", [P, F], F32R)
        t32 = sb("t32", [P, F])
        prod = sb("prod", [P, F])
        w_raw = sb("w_raw", [P, 1])
        w_col = sb("w_col", [P, 1])
        neg_max = sb("neg_max", [P, 1])
        e_row = sb("e_row", [P, N])
        e_sum = sb("e_sum", [P, 1])
        e_col = sb("e_col", [P, 1])
        e_inv = sb("e_inv", [P, 1])
        p_col = sb("p_col", [P, 1])
        y = sb("y", [P, 2, F])

        bank = [ctx.enter_context(nc.psum_tensor(f"bank{n}", [P, 512], F32)) for n in range(8)]
        A0, B0, A1, B1, A2, B2, A3, B3 = bank

        (gate0_in, attn_in, mask_in, k_in, bk_in, rows_in, w1_in, w2_in, qk_in, v_in) = [sem(n) for n in (
            "gate0_in", "attn_in", "mask_in", "k_in", "bk_in", "rows_in", "w1_in", "w2_in", "qk_in", "v_in")]
        (ident_zero, ident_done, consts_done, attn_products, k2u_filled, scaled_products, w2_scaled,
         mv_filled, bias_summed, bias_hi_done, bias_done, spread_done,
         columns_done) = [sem(n) for n in (
             "ident_zero", "ident_done", "consts_done", "attn_products", "k2u_filled",
             "scaled_products", "w2_scaled", "mv_filled", "bias_summed", "bias_hi_done", "bias_done",
             "spread_done", "columns_done")]
        part_hi = {name: sem(f"{name}_hi_done") for name in at}
        part_split = {name: sem(f"{name}_split") for name in at}
        x_loaded = [sem(f"x_loaded{i}") for i in range(SLOTS)]
        adj_loaded = [sem(f"adj_loaded{i}") for i in range(SLOTS)]
        adj_t_loaded = [sem(f"adj_t_loaded{i}") for i in range(SLOTS)]
        y_stored = [sem(f"y_stored{i}") for i in range(2)]
        stats_done = [sem(f"stats_done{i}") for i in range(5)]
        aggr_done = [sem(f"aggr_done{i}") for i in range(5)]
        var_done = [sem(f"var_done{i}") for i in range(5)]
        rstd_done = [sem(f"rstd_done{i}") for i in range(5)]
        shift_done = [sem(f"shift_done{i}") for i in range(5)]
        names = """adjm_done deg_done deg_clamped deg_ready adjn_done h0_done l0_transposed l0_copied inc_done
            binv_clamped binv_done bhi_done blo_done binc_done l0_split gates_done gb_copied
            s_done s_copied dclamp_done drec_done dinv_done d_done agg_done x1_done h1_done
            h1_transposed h1_hi_done h1_split g2s_done g10_done g2s_copied si_done sj_spread
            exp_max_done exp_done alpha_done row_eps_done row_inv_done trans_done trans_transposed
            trans_copied hop1_done q1_done hop2_done x2_done h2_done x2b_done base_h_done
            base_r_done base_done sh_done sh_hi_done sh_split w1_done r0_done r1_done zn_done
            sz_done sz_hi_done sz_split w2_done x3_done h3_done h3_transposed h3_hi_done h3_split
            agg3_done tv_done t_copied w_raw_done w_done w_spread max_done e_row_done e_col_done
            e_inv_done p_done y_done""".split()
        S = {n: sem(n) for n in names}
        (adjm_done, deg_done, deg_clamped, deg_ready, adjn_done, h0_done, l0_transposed, l0_copied, inc_done,
         binv_clamped, binv_done, bhi_done, blo_done, binc_done, l0_split, gates_done, gb_copied,
         s_done, s_copied, dclamp_done, drec_done, dinv_done, d_done, agg_done, x1_done, h1_done,
         h1_transposed, h1_hi_done, h1_split, g2s_done, g10_done, g2s_copied, si_done, sj_spread,
         exp_max_done, exp_done, alpha_done, row_eps_done, row_inv_done, trans_done, trans_transposed,
         trans_copied, hop1_done, q1_done, hop2_done, x2_done, h2_done, x2b_done, base_h_done,
         base_r_done, base_done, sh_done, sh_hi_done, sh_split, w1_done, r0_done, r1_done, zn_done,
         sz_done, sz_hi_done, sz_split, w2_done, x3_done, h3_done, h3_transposed, h3_hi_done,
         h3_split, agg3_done, tv_done, t_copied, w_raw_done, w_done, w_spread, max_done, e_row_done,
         e_col_done, e_inv_done, p_done, y_done) = [S[n] for n in names]

        def loaded(eng, sems, g):
            count = ((g.n - g.s) // SLOTS + 1) * 16 if isinstance(g.n, int) else (g.n - g.s) * 4 + 16
            eng.wait_ge(sems[g.s], count)

        block = ctx.enter_context(nc.Block())

        @block.sync
        def _(sp):
            def c(ap, chunks):
                return ap.rearrange("(c p) n -> p c n", c=chunks)

            def on_all(v):
                return v.rearrange("(a n) -> a n", a=1).to_broadcast([P, v.shape[0]])

            def load_weights(loads):
                for dst, src, done in loads:
                    sp.dma_start(dst, src).then_inc(done, 16)

            def setup_layer0():
                load_weights([(gate0[0][:, :, 0:F], c(w0t[F:2 * F, :], FC), gate0_in),
                              (gate0[0][:, :, F:2 * F], c(w0t[0:F, :], FC), gate0_in)])

            def setup_layer1():
                load_weights([(wv1_sb[:], c(wv1t, FC), attn_in), (aw_sb[:], aw, attn_in),
                              (bv_sb[:], bv, attn_in), (ab_sb[:], on_all(ab), attn_in),
                              (k2u[0][:, :, 0:F], c(wk[2], FC), k_in),
                              (k10[0][:, :, 0:F], c(wk[1], FC), k_in),
                              (k10[0][:, :, F:2 * F], c(wk[0], FC), k_in),
                              (mask_sb[:], mask_t, mask_in)]
                             + [(bk3[:, k, :], bk[k:k + 1, :].to_broadcast([P, F]), bk_in) for k in range(K)])

            def setup_others():
                load_weights([(w1[0], c(w1t, FC), w1_in), (gamma_sb[:], gamma, w2_in),
                              (beta_sb[:], beta, w2_in), (w2_raw[:], c(w2t, HC), w2_in),
                              (b1_rows[:], on_all(b1), rows_in), (b2_rows[:], on_all(b2), rows_in),
                              (wqk_sb[:], c(wqk_t, 2 * FC), qk_in),
                              (mv[0][:, :, F:2 * F], c(wv3, FC), v_in)])

            def load(g):
                wait(sp, x1_done, g.n - SLOTS + 1)
                sp.dma_start(x_in[:, g.s, :], x[g.n]).then_inc(x_loaded[g.s], 16)
                wait(sp, adjm_done, g.n - SLOTS + 1)
                wait(sp, blo_done, g.n - SLOTS + 1)
                sp.dma_start(adj_t[:, g.s, 1:1 + N], adj_tr[g.n]).then_inc(adj_t_loaded[g.s], 16)
                wait(sp, deg_done, g.n - SLOTS + 1)
                wait(sp, adjn_done, g.n - SLOTS + 1)
                wait(sp, alpha_done, g.n - SLOTS + 1)
                sp.dma_start(adj_in[:, g.s, :], adj[g.n]).then_inc(adj_loaded[g.s], 16)

            def store(g):
                wait(sp, y_done, g.n + 1)
                sp.dma_start(out[g.n], y[:, g.s2, :]).then_inc(y_stored[g.s2], 16)

            def step(t, k):
                if (g := in_flight(t, k, 0, G)):
                    load(g)
                if (g := in_flight(t, k, DEPTH + 1, G)):
                    store(g)

            run_steps(sp, step, G, (setup_layer0, setup_layer1, setup_others))
            for i in range(2):
                sp.wait_ge(y_stored[i], 16 * G // 2)

        @block.gpsimd
        def _(pool):
            pool.memset(minus_half[:], -0.5)
            pool.memset(ones_zeros[:, 0:1], 1.0)
            pool.memset(ones_zeros[:, 1:2], 0.0)
            pool.memset(spread32[:], 2.0 / P).then_inc(consts_done, 1)
            pool.memset(ident[:], 0.0).then_inc(ident_zero, 1)
            pool.wait_ge(ident_zero, 1)
            pool.affine_select(out=ident[:], in_=ident[:], compare_op=ALU.not_equal, fill=1.0, base=0,
                               pattern=[[-1, P]], channel_multiplier=1).then_inc(ident_done, 1)
            pool.wait_ge(consts_done, 1)

            def rstd_of(n, g):
                pool.wait_ge(var_done[n], g.n + 1)
                r = rstd[n][:, g.s:g.s + 1]
                pool.tensor_tensor(r, var_eps[n][:, g.s:g.s + 1], minus_half[:], ALU.pow)\
                    .then_inc(rstd_done[n], 1)

            def shift_of(n, g):
                constant_wait(pool, consts_done)
                pool.wait_ge(rstd_done[n], g.n + 1)
                pool.tensor_scalar(shift[n][:, g.s:g.s + 1], mean_var[n][:, g.s, 0:1],
                                   rstd[n][:, g.s:g.s + 1], -1.0, ALU.mult, ALU.mult)\
                    .then_inc(shift_done[n], 1)

            rstd0, rstd1, rstd2, rstd3, rstd4 = [lambda g, n=n: rstd_of(n, g) for n in range(5)]
            shift0, shift1, shift2, shift3, shift4 = [lambda g, n=n: shift_of(n, g) for n in range(5)]

            def base_x(g):
                first_use(pool, g, rows_in, 16 * 2)
                pool.wait_ge(x2_done, g.n + 1)
                pool.tensor_tensor(x2b[:, g.s2, :], x2[:, g.s, :], b2_rows[:], ALU.add)\
                    .then_inc(x2b_done, 1)

            def base_beta(g):
                first_use(pool, g, w2_scaled, 1)
                constant_wait(pool, consts_done)
                pool.wait_ge(d_done, g.n + 1)
                pool.tensor_scalar(base_r[:, g.s2, :], beta_w2[:], rho[:, g.s:g.s + 1], 1.0, ALU.mult, ALU.mult)\
                    .then_inc(base_r_done, 1)

            def base_h2(g):
                pool.wait_ge(h2_done, g.n + 1)
                pool.wait_ge(x2b_done, g.n + 1)
                pool.tensor_tensor(base_h[:, g.s2, :], x2b[:, g.s2, :], h2[:, g.s, :], ALU.add)\
                    .then_inc(base_h_done, 1)

            def base_sum(g):
                pool.wait_ge(base_h_done, g.n + 1)
                pool.wait_ge(base_r_done, g.n + 1)
                pool.tensor_tensor(base[:, g.s, :], base_h[:, g.s2, :], base_r[:, g.s2, :], ALU.add)\
                    .then_inc(base_done, 1)

            def step(t, k):
                for piece, back in ((shift0, 1), (base_x, 4), (rstd1, 2), (base_h2, 4), (shift1, 2),
                    (base_sum, 4), (rstd4, 4), (shift4, 4), (rstd2, 3), (shift2, 3), (base_beta, 3),
                    (rstd0, 0), (rstd3, 5), (shift3, 5)):
                    if (g := in_flight(t, k, back, G)):
                        piece(g)

            run_steps(pool, step, G)

        @block.scalar
        def _(act):
            def hi(name):
                cols = slice(*at[name])
                act.activation(w_hi[:, cols], w32[:, cols], ACT.Copy).then_inc(part_hi[name], 1)

            def setup_layer0():
                act.wait_ge(consts_done, 1)
                for slot in range(2):
                    act.activation(edge_hi[:, slot, 2:3], ones_zeros[:, 0:1], ACT.Copy)
                    last = act.activation(edge_lo[:, slot, 2:3], ones_zeros[:, 1:2], ACT.Copy)
                last.then_inc(columns_done, 1)
                act.wait_ge(gate0_in, 16 * 2)
                hi("gate0")

            def setup_layer1():
                act.wait_ge(k_in, 16 * 3)
                hi("k10")
                act.wait_ge(k2u_filled, 1)
                hi("k2u")
                act.wait_ge(bias_summed, 2)
                act.activation(bk_hi[:], bk_sum[:], ACT.Copy).then_inc(bias_hi_done, 1)
                act.activation(spread[:], spread32[:], ACT.Copy).then_inc(spread_done, 1)

            def setup_hidden():
                act.wait_ge(w1_in, 16)
                hi("w1")

            def setup_out():
                act.wait_ge(w2_scaled, 1)
                hi("w2")

            def setup_layer3():
                act.wait_ge(mv_filled, 1)
                act.wait_ge(v_in, 16)
                hi("mv")

            def norm(n, g, dst, src, done, func=ACT.Relu):
                act.wait_ge(shift_done[n], g.n + 1)
                act.activation(dst, src, func, bias=shift[n][:, g.s:g.s + 1],
                               scale=rstd[n][:, g.s:g.s + 1]).then_inc(done, 1)

            def adj_normalised(g):
                act.wait_ge(deg_ready, g.n + 1)
                act.activation(adj_norm[:, g.s2, :], adj_in[:, g.s, :], ACT.Copy,
                               scale=deg_inv[:, g.s2:g.s2 + 1]).then_inc(adjn_done, 1)

            def norm0(g):
                norm(0, g, h0[:, g.s2, :], x_in[:, g.s, :], h0_done)

            def adjm(g):
                first_use(act, g, mask_in, 16)
                loaded(act, adj_t_loaded, g)
                act.activation(adjm_t[:, g.s, :], adj_t[:, g.s, 1:1 + N], ACT.Copy,
                               scale=mask_sb[:, bass.ds(g.n, 1)]).then_inc(adjm_done, 1)

            def l0_copies(g):
                act.wait_ge(l0_transposed, g.n + 1)
                act.activation(adjn_t[:, g.s2, :], A0[:, 0:N], ACT.Copy)
                act.activation(h0t_hi[:], A0[:, N:N + F], ACT.Copy).then_inc(l0_copied, 1)

            def edge_scale(g):
                act.wait_ge(blo_done, g.n + 1)
                wait(act, s_done, g.n - 1)
                inc32 = inc_t[:, g.s2, :].bitcast(F32)
                act.activation(edge_hi[:, g.s2, 3:3 + N], inc32, ACT.Copy,
                               scale=edge_hi[:, g.s2, 0:1].bitcast(F32))
                act.activation(edge_lo[:, g.s2, 3:3 + N], inc32, ACT.Copy,
                               scale=edge_lo[:, g.s2, 0:1].bitcast(F32)).then_inc(binc_done, 1)

            def gb_copy(g):
                act.wait_ge(gates_done, g.n + 1)
                act.activation(gb[:], B0[:, 0:F], ACT.Copy).then_inc(gb_copied, 1)

            def s_copy(g):
                act.wait_ge(s_done, g.n + 1)
                act.activation(s_sums[:, g.s, :], A0[:, 0:2 + N], ACT.Copy).then_inc(s_copied, 1)

            def norm1(g):
                norm(1, g, h1[:], x1[:, g.s, :], h1_done)

            def h1_hi(g):
                act.wait_ge(h1_transposed, g.n + 1)
                act.activation(h1t_hi[:], A1[:, 0:F], ACT.Copy).then_inc(h1_hi_done, 1)

            def g2s_copy(g):
                act.wait_ge(g2s_done, g.n + 1)
                act.activation(g2s[:], B1[:, 0:F + 2], ACT.Copy).then_inc(g2s_copied, 1)

            def scores(g):
                act.wait_ge(sj_spread, g.n + 1)
                act.wait_ge(si_done, g.n + 1)
                act.activation(z_exp[:], B1[:, 0:N], ACT.Exp, bias=si[:, 0:1])
                act.activation(B1[:, N:2 * N], B1[:, 0:N], ACT.Exp, bias=si[:, 1:2], scale=0.2)\
                    .then_inc(exp_done, 1)

            def trans_copy(g):
                act.wait_ge(trans_transposed, g.n + 1)
                act.activation(trans_t[:], B1[:, 0:N], ACT.Copy).then_inc(trans_copied, 1)

            def q1_copy(g):
                act.wait_ge(hop1_done, g.n + 1)
                act.activation(q1[:], A1[:, 0:F], ACT.Copy).then_inc(q1_done, 1)

            def norm2(g):
                norm(2, g, h2[:, g.s, :], x2[:, g.s, :], h2_done)

            def sh_hi_copy(g):
                act.wait_ge(sh_done, g.n + 1)
                act.activation(sh_hi[:], A2[:, 0:F], ACT.Copy).then_inc(sh_hi_done, 1)

            def hidden_relu(g):
                act.wait_ge(r0_done, g.n + 1)
                act.activation(r1[:], r0[:], ACT.Relu).then_inc(r1_done, 1)

            def norm4(g):
                norm(4, g, zn[:], r1[:], zn_done, ACT.Identity)

            def sz_hi_copy(g):
                act.wait_ge(sz_done, g.n + 1)
                act.activation(sz_hi[:], A2[:, 0:H], ACT.Copy).then_inc(sz_hi_done, 1)

            def norm3(g):
                norm(3, g, h3[:, g.s2, :], x3[:, g.s, :], h3_done)

            def h3_hi(g):
                act.wait_ge(h3_transposed, g.n + 1)
                act.activation(h3t_hi[:], A3[:, 0:F], ACT.Copy).then_inc(h3_hi_done, 1)

            def t_copy(g):
                act.wait_ge(tv_done, g.n + 1)
                act.activation(t32[:], B3[:, 0:F], ACT.Copy).then_inc(t_copied, 1)

            def softmax(g):
                act.wait_ge(max_done, g.n + 1)
                act.activation(e_row[:], A3[:, 0:N], ACT.Exp, bias=neg_max[:], accum_out=e_sum[:])\
                    .then_inc(e_row_done, 1)
                act.activation(e_col[:], w_col[:], ACT.Exp, bias=neg_max[:]).then_inc(e_col_done, 1)

            def step(t, k):
                for piece, back in ((h3_hi, 6), (l0_copies, 1), (q1_copy, 3), (norm1, 2),
                    (hidden_relu, 4), (h1_hi, 2), (edge_scale, 1), (t_copy, 6), (gb_copy, 1),
                    (adj_normalised, 0), (norm4, 4), (g2s_copy, 2), (norm2, 3), (sz_hi_copy, 4),
                    (adjm, 3), (scores, 2), (s_copy, 1), (softmax, 6), (sh_hi_copy, 3), (norm0, 0),
                    (norm3, 5), (trans_copy, 2)):
                    if (g := in_flight(t, k, back, G)):
                        piece(g)

            run_steps(act, step, G, (setup_layer0, setup_layer1, setup_hidden, setup_out, setup_layer3))

        @block.vector
        def _(dve):
            def lo(name):
                cols = slice(*at[name])
                dve.wait_ge(part_hi[name], 1)
                dve.tensor_tensor(w_lo[:, cols], w32[:, cols], w_hi[:, cols].bitcast(F32), ALU.subtract)\
                    .then_inc(part_split[name], 1)

            def setup_layer0():
                dve.wait_ge(gate0_in, 16 * 2)
                lo("gate0")

            def setup_layer1():
                dve.wait_ge(bk_in, 16 * K)
                dve.tensor_tensor(bk_sum[:], bk3[:, 0, :], bk3[:, 1, :], ALU.add)\
                    .then_inc(bias_summed, 1)
                dve.wait_ge(bias_summed, 1)
                dve.tensor_tensor(bk_sum[:], bk_sum[:], bk3[:, 2, :], ALU.add).then_inc(bias_summed, 1)
                dve.wait_ge(attn_in, 16 * 4)
                dve.wait_ge(attn_products, 1)
                dve.tensor_copy(k2u[0][:, :, F:F + 2], B3[:, 0:2 * FC].rearrange("p (c n) -> p c n", c=FC))
                dve.tensor_tensor(score_bias[:], B3[:, 2 * FC:2 * FC + 1], ab_sb[:], ALU.add)\
                    .then_inc(k2u_filled, 1)
                dve.wait_ge(k2u_filled, 1)
                dve.wait_ge(k_in, 16 * 3)
                lo("k10")
                lo("k2u")
                dve.wait_ge(bias_hi_done, 1)
                dve.tensor_copy(bias_rows[0:P // 2, :], bk_hi[0:P // 2, :].bitcast(F32))
                dve.tensor_tensor(bias_rows[P // 2:P, :], bk_sum[P // 2:P, :], bk_hi[P // 2:P, :].bitcast(F32),
                                  ALU.subtract).then_inc(bias_done, 1)

            def setup_hidden():
                dve.wait_ge(w1_in, 16)
                lo("w1")
                dve.wait_ge(mask_in, 16)
                dve.tensor_scalar(mask_scaled[:], mask_sb[:], SCORE_SCALE, None, ALU.mult)

            def setup_out():
                dve.wait_ge(w2_in, 16 * 3)
                for c in range(HC):
                    dve.tensor_scalar(w2[0][:, c, :], w2_raw[:, c, :], gamma_sb[:, c:c + 1], None, ALU.mult)
                dve.wait_ge(scaled_products, 1)
                dve.tensor_copy(mv[0][:, :, 0:F], A3[:].rearrange("p (c n) -> p c n", c=FC))\
                    .then_inc(mv_filled, 1)
                dve.tensor_copy(beta_w2[:], B3[:, F:2 * F]).then_inc(w2_scaled, 1)
                dve.wait_ge(w2_scaled, 1)
                lo("w2")
                dve.wait_ge(rows_in, 16 * 2)

            def setup_layer3():
                dve.wait_ge(v_in, 16)
                dve.wait_ge(mv_filled, 1)
                lo("mv")

            def norm_stats(n, g, src, src_done):
                if src_done is None:
                    loaded(dve, x_loaded, g)
                else:
                    dve.wait_ge(src_done, g.n + 1)
                dve.bn_stats(stats[n][:], src).then_inc(stats_done[n], 1)

            def norm_mean(n, g):
                constant_wait(dve, consts_done)
                dve.wait_ge(stats_done[n], g.n + 1)
                dve.bn_aggr(mean_var[n][:, g.s, :], stats[n][:]).then_inc(aggr_done[n], 1)

            def norm_eps(n, g):
                dve.wait_ge(aggr_done[n], g.n + 1)
                dve.tensor_scalar(var_eps[n][:, g.s:g.s + 1], mean_var[n][:, g.s, 1:2], EPS, None, ALU.add)\
                    .then_inc(var_done[n], 1)

            def stats0(g):
                dve.wait_ge(deg_done, g.n + 1)
                norm_stats(0, g, x_in[:, g.s, :], None)

            def stats1(g):
                norm_stats(1, g, x1[:, g.s, :], x1_done)

            def stats2(g):
                norm_stats(2, g, x2[:, g.s, :], x2_done)

            def stats3(g):
                norm_stats(3, g, x3[:, g.s, :], x3_done)

            def stats4(g):
                norm_stats(4, g, r1[:], r1_done)

            mean0, mean1, mean2, mean3, mean4 = [lambda g, n=n: norm_mean(n, g) for n in range(5)]
            eps0, eps1, eps2, eps3, eps4 = [lambda g, n=n: norm_eps(n, g) for n in range(5)]

            def degree(g):
                loaded(dve, adj_loaded, g)
                dve.tensor_reduce(deg[:, g.s2:g.s2 + 1], adj_in[:, g.s, :], AX.X, ALU.add)\
                    .then_inc(deg_done, 1)

            def degree_clamp(g):
                dve.wait_ge(deg_done, g.n + 1)
                dve.tensor_scalar(deg_max[:, g.s2:g.s2 + 1], deg[:, g.s2:g.s2 + 1], 1e-6, None, ALU.max)\
                    .then_inc(deg_clamped, 1)

            def degree_inv(g):
                dve.wait_ge(deg_clamped, g.n + 1)
                wait(dve, adjn_done, g.n - 1)
                dve.reciprocal(deg_inv[:, g.s2:g.s2 + 1], deg_max[:, g.s2:g.s2 + 1])\
                    .then_inc(deg_ready, 1)

            def h0_lo(g):
                dve.wait_ge(l0_copied, g.n + 1)
                dve.tensor_tensor(h0t_lo[:], A0[:, N:N + F], h0t_hi[:].bitcast(F32), ALU.subtract)\
                    .then_inc(l0_split, 1)

            def incidence(g):
                loaded(dve, adj_t_loaded, g)
                wait(dve, s_done, g.n - 1)
                dve.tensor_scalar(inc_t[:, g.s2, :], adj_t[:, g.s, 1:1 + N], 0.0, None, ALU.not_equal, ALU.add,
                                  accum_out=edge_size[:, g.s2:g.s2 + 1]).then_inc(inc_done, 1)

            def edge_clamp(g):
                dve.wait_ge(inc_done, g.n + 1)
                dve.tensor_scalar(edge_max[:, g.s2:g.s2 + 1], edge_size[:, g.s2:g.s2 + 1], 1.0, None, ALU.max)\
                    .then_inc(binv_clamped, 1)

            def edge_inv(g):
                dve.wait_ge(binv_clamped, g.n + 1)
                dve.reciprocal(adj_t[:, g.s, 0:1], edge_max[:, g.s2:g.s2 + 1]).then_inc(binv_done, 1)

            def edge_hi_part(g):
                dve.wait_ge(binv_done, g.n + 1)
                wait(dve, s_done, g.n - 1)
                dve.tensor_copy(edge_hi[:, g.s2, 0:2], adj_t[:, g.s, 0:2]).then_inc(bhi_done, 1)

            def edge_lo_part(g):
                dve.wait_ge(bhi_done, g.n + 1)
                dve.tensor_tensor(edge_lo[:, g.s2, 0:2], adj_t[:, g.s, 0:2],
                                  edge_hi[:, g.s2, 0:2].bitcast(F32), ALU.subtract).then_inc(blo_done, 1)

            def node_clamp(g):
                dve.wait_ge(s_copied, g.n + 1)
                dve.tensor_scalar(d_max[:, g.s2:g.s2 + 1], s_sums[:, g.s, 0:1], 1.1754944e-38, None, ALU.max)\
                    .then_inc(dclamp_done, 1)

            def node_rec(g):
                dve.wait_ge(dclamp_done, g.n + 1)
                dve.reciprocal(d_rec[:, g.s2:g.s2 + 1], d_max[:, g.s2:g.s2 + 1]).then_inc(drec_done, 1)

            def node_inv(g):
                dve.wait_ge(drec_done, g.n + 1)
                dve.scalar_tensor_tensor(d_inv[:, g.s:g.s + 1], s_sums[:, g.s, 0:1], 0.0, d_rec[:, g.s2:g.s2 + 1],
                                         ALU.is_gt, ALU.mult).then_inc(dinv_done, 1)

            def node_rho(g):
                dve.wait_ge(dinv_done, g.n + 1)
                dve.tensor_tensor(rho[:, g.s:g.s + 1], s_sums[:, g.s, 1:2], d_inv[:, g.s:g.s + 1], ALU.mult)\
                    .then_inc(d_done, 1)

            def x1_sum(g):
                dve.wait_ge(agg_done, g.n + 1)
                dve.scalar_tensor_tensor(x1[:, g.s, :], B0[:, F:2 * F], 0.0, x_in[:, g.s, :],
                                         ALU.max, ALU.add).then_inc(x1_done, 1)

            def h1_lo(g):
                dve.wait_ge(h1_hi_done, g.n + 1)
                dve.tensor_tensor(h1t_lo[:], A1[:, 0:F], h1t_hi[:].bitcast(F32), ALU.subtract)\
                    .then_inc(h1_split, 1)

            def si_add(g):
                dve.wait_ge(g2s_copied, g.n + 1)
                dve.tensor_scalar(si[:, 0:1], g2s[:, F + 1:F + 2], score_bias[:], None, ALU.add)
                dve.tensor_scalar(si[:, 1:2], g2s[:, F + 1:F + 2], score_bias[:], 0.2, ALU.add, ALU.mult)\
                    .then_inc(si_done, 1)

            def exp_max(g):
                dve.wait_ge(exp_done, g.n + 1)
                dve.tensor_tensor(z_max[:], B1[:, N:2 * N], z_exp[:], ALU.max).then_inc(exp_max_done, 1)

            def attention(g):
                dve.wait_ge(exp_max_done, g.n + 1)
                dve.tensor_tensor_reduce(alpha[:], z_max[:], adj_in[:, g.s, :], 1.0, 0.0, ALU.mult,
                                         ALU.add, row_sum[:]).then_inc(alpha_done, 1)

            def attention_eps(g):
                dve.wait_ge(alpha_done, g.n + 1)
                dve.tensor_scalar(row_eps[:], row_sum[:], 1e-12, None, ALU.add).then_inc(row_eps_done, 1)

            def attention_inv(g):
                dve.wait_ge(row_eps_done, g.n + 1)
                dve.reciprocal(row_inv[:], row_eps[:]).then_inc(row_inv_done, 1)

            def transition(g):
                dve.wait_ge(row_inv_done, g.n + 1)
                dve.tensor_scalar(trans[:], alpha[:], row_inv[:], None, ALU.mult).then_inc(trans_done, 1)

            def x2_sum(g):
                dve.wait_ge(hop2_done, g.n + 1)
                dve.scalar_tensor_tensor(x2[:, g.s, :], A1[:, F:2 * F], 0.0, x1[:, g.s, :],
                                         ALU.max, ALU.add).then_inc(x2_done, 1)

            def sh_lo_part(g):
                dve.wait_ge(sh_hi_done, g.n + 1)
                dve.tensor_tensor(sh_lo[:], A2[:, 0:F], sh_hi[:].bitcast(F32), ALU.subtract)\
                    .then_inc(sh_split, 1)

            def hidden(g):
                dve.wait_ge(w1_done, g.n + 1)
                dve.scalar_tensor_tensor(r0[:], B2[:, 0:H], d_inv[:, g.s:g.s + 1], b1_rows[:],
                                         ALU.mult, ALU.add).then_inc(r0_done, 1)

            def sz_lo_part(g):
                dve.wait_ge(sz_hi_done, g.n + 1)
                dve.tensor_tensor(sz_lo[:], A2[:, 0:H], sz_hi[:].bitcast(F32), ALU.subtract)\
                    .then_inc(sz_split, 1)

            def x3_sum(g):
                dve.wait_ge(w2_done, g.n + 1)
                dve.wait_ge(base_done, g.n + 1)
                dve.scalar_tensor_tensor(x3[:, g.s, :], B2[:, 0:F], d_inv[:, g.s:g.s + 1],
                                         base[:, g.s, :], ALU.mult, ALU.add).then_inc(x3_done, 1)

            def h3_lo(g):
                dve.wait_ge(h3_hi_done, g.n + 1)
                dve.tensor_tensor(h3t_lo[:], A3[:, 0:F], h3t_hi[:].bitcast(F32), ALU.subtract)\
                    .then_inc(h3_split, 1)

            def gate(g):
                dve.wait_ge(agg3_done, g.n + 1)
                dve.wait_ge(t_copied, g.n + 1)
                dve.tensor_tensor_reduce(prod[:], A3[:, 0:F], t32[:], 1.0, 0.0, ALU.mult, ALU.add,
                                         w_raw[:]).then_inc(w_raw_done, 1)

            def gate_scale(g):
                dve.wait_ge(w_raw_done, g.n + 1)
                dve.tensor_scalar(w_col[:], w_raw[:], mask_scaled[:, bass.ds(g.n, 1)], None, ALU.mult)\
                    .then_inc(w_done, 1)

            def row_max(g):
                dve.wait_ge(w_spread, g.n + 1)
                dve.tensor_reduce(neg_max[:], A3[:, 0:N], AX.X, ALU.max, negate=True)\
                    .then_inc(max_done, 1)

            def softmax_inv(g):
                dve.wait_ge(e_row_done, g.n + 1)
                dve.reciprocal(e_inv[:], e_sum[:]).then_inc(e_inv_done, 1)

            def softmax_p(g):
                dve.wait_ge(e_inv_done, g.n + 1)
                dve.wait_ge(e_col_done, g.n + 1)
                dve.tensor_tensor(p_col[:], e_col[:], e_inv[:], ALU.mult).then_inc(p_done, 1)

            def result(g):
                dve.wait_ge(p_done, g.n + 1)
                if not isinstance(g.n, int):
                    dve.wait_ge(y_stored[g.s2], (g.n - g.s2) * 8)
                elif g.n >= 2:
                    dve.wait_ge(y_stored[g.s2], g.n // 2 * 16)
                dve.scalar_tensor_tensor(y[:, g.s2, :], B3[:, F:2 * F], p_col[:], x3[:, g.s, :],
                                         ALU.mult, ALU.add).then_inc(y_done, 1)

            def step(t, k):
                for piece, back in ((incidence, 0), (degree, 0), (edge_clamp, 0), (node_rec, 2),
                    (h3_lo, 6), (degree_clamp, 0), (h0_lo, 1), (stats3, 5), (hidden, 4), (x2_sum, 3),
                    (mean3, 5), (stats0, 0), (stats4, 4), (edge_inv, 0), (node_inv, 2), (mean4, 4),
                    (degree_inv, 0), (eps4, 4), (eps3, 5), (stats2, 3), (h1_lo, 2), (mean0, 0),
                    (mean2, 3), (edge_hi_part, 0), (eps2, 3), (gate, 6), (gate_scale, 6), (eps0, 0),
                    (x1_sum, 1), (node_rho, 2), (si_add, 2), (stats1, 1), (row_max, 6), (sz_lo_part, 4),
                    (exp_max, 2), (mean1, 1), (edge_lo_part, 0), (attention, 2), (attention_eps, 2),
                    (attention_inv, 2), (softmax_inv, 6), (node_clamp, 1), (transition, 2), (eps1, 1),
                    (softmax_p, 6), (sh_lo_part, 3), (result, 6), (x3_sum, 4)):
                    if (g := in_flight(t, k, back, G)):
                        piece(g)

            run_steps(dve, step, G, (setup_layer0, setup_layer1, setup_hidden, setup_out, setup_layer3))

        @block.tensor
        def _(pe):
            def group(dst, pairs, start=True, stop=True):
                for i, (a, b) in enumerate(pairs):
                    mm = pe.matmul(dst, a, b, start=start and i == 0, stop=stop and i == len(pairs) - 1,
                                   skip_group_check=not (start and stop))
                return mm

            def split_pairs(a_hi, a_lo, w, c):
                return [(a_hi, w[1][:, c, :]), (a_hi, w[2][:, c, :]), (a_lo, w[1][:, c, :])]

            def by_weight(dst, hi, lo, w, chunks, stop=True):
                pairs = []
                for c in range(chunks):
                    pairs += split_pairs(hi[:, c * P:(c + 1) * P], lo[:, c * P:(c + 1) * P], w, c)
                return group(dst, pairs, stop=stop)

            def setup_layer1():
                pe.wait_ge(attn_in, 16 * 4)
                for f in range(FC):
                    rows = slice(f * P, (f + 1) * P)
                    group(B3[:, 2 * f:2 * f + 2], [(wv1_sb[:, d, rows], aw_sb[:, d, :]) for d in range(FC)])
                group(B3[:, 2 * FC:2 * FC + 1],
                      [(bv_sb[:, d:d + 1].to_broadcast([P, P]), aw_sb[:, d, i:i + 1])
                       for d in range(FC) for i in range(2)]).then_inc(attn_products, 1)

            def setup_out():
                pe.wait_ge(k2u_filled, 1)
                pe.wait_ge(qk_in, 16)
                pe.wait_ge(w2_in, 16 * 3)
                for f in range(FC):
                    rows = slice(f * P, (f + 1) * P)
                    group(A3[:, f * F:(f + 1) * F],
                          [(wqk_sb[:, d, rows], wqk_sb[:, FC + d, :]) for d in range(FC)])
                group(B3[:, F:2 * F], [(beta_sb[:, c:c + 1].to_broadcast([P, P]), w2_raw[:, c, :])
                                       for c in range(HC)]).then_inc(scaled_products, 1)

            pe.wait_ge(ident_done, 1)
            pe.wait_ge(columns_done, 1)

            def l0_transposes(g):
                pe.wait_ge(h0_done, g.n + 1)
                pe.wait_ge(adjn_done, g.n + 1)
                wait(pe, s_copied, g.n)
                pe.transpose(A0[:, 0:N], adj_norm[:, g.s2, :], ident[:])
                for c in range(FC):
                    mm = pe.transpose(A0[:, N + c * P:N + (c + 1) * P],
                                      h0[:, g.s2, c * P:(c + 1) * P], ident[:])
                mm.then_inc(l0_transposed, 1)

            def l0_gates(g):
                first_use(pe, g, part_split["gate0"], 1)
                pe.wait_ge(l0_split, g.n + 1)
                wait(pe, x1_done, g.n)
                by_weight(B0[:, :], h0t_hi, h0t_lo, gate0, FC, stop=False).then_inc(gates_done, 1)

            def l0_incidence(g):
                pe.wait_ge(binc_done, g.n + 1)
                pe.wait_ge(l0_split, g.n + 1)
                inc = inc_t[:, g.s2, :]
                group(A0[:, 0:2 + N], [(inc, edge_hi[:, g.s2, 1:3 + N]), (inc, edge_lo[:, g.s2, 1:3 + N])])\
                    .then_inc(s_done, 1)

            def l0_aggregate(g):
                pe.wait_ge(gb_copied, g.n + 1)
                group(B0[:, F:2 * F], [(adjn_t[:, g.s2, :], gb[:])], start=False).then_inc(agg_done, 1)

            def h1_transposes(g):
                pe.wait_ge(h1_done, g.n + 1)
                wait(pe, x2_done, g.n)
                for c in range(FC):
                    mm = pe.transpose(A1[:, c * P:(c + 1) * P], h1[:, c * P:(c + 1) * P], ident[:])
                mm.then_inc(h1_transposed, 1)

            def l1_product2(g):
                first_use(pe, g, part_split["k2u"], 1)
                pe.wait_ge(h1_split, g.n + 1)
                by_weight(B1[:, 0:F + 2], h1t_hi, h1t_lo, k2u, FC).then_inc(g2s_done, 1)

            def l1_products10(g):
                first_use(pe, g, part_split["k10"], 1)
                first_use(pe, g, bias_done, 1)
                first_use(pe, g, spread_done, 1)
                pe.wait_ge(h1_split, g.n + 1)
                by_weight(A1[:, :], h1t_hi, h1t_lo, k10, FC, stop=False)
                group(A1[:, F:2 * F], [(spread[:], bias_rows[:])], start=False, stop=False)\
                    .then_inc(g10_done, 1)

            def l1_spread(g):
                pe.wait_ge(g2s_copied, g.n + 1)
                pe.transpose(B1[:, 0:N], g2s[:, F:F + 1].to_broadcast([P, N]), ident[:])\
                    .then_inc(sj_spread, 1)

            def l1_transpose(g):
                pe.wait_ge(trans_done, g.n + 1)
                pe.transpose(B1[:, 0:N], trans[:], ident[:]).then_inc(trans_transposed, 1)

            def l1_hop1(g):
                pe.wait_ge(trans_copied, g.n + 1)
                group(A1[:, 0:F], [(trans_t[:], g2s[:, 0:F])], start=False, stop=False)\
                    .then_inc(hop1_done, 1)

            def l1_hop2(g):
                pe.wait_ge(q1_done, g.n + 1)
                group(A1[:, F:2 * F], [(trans_t[:], q1[:])], start=False).then_inc(hop2_done, 1)

            def l2_smooth(g):
                wait(pe, sz_split, g.n)
                pe.wait_ge(h2_done, g.n + 1)
                pe.wait_ge(s_copied, g.n + 1)
                for c in range(FC):
                    mm = group(A2[:, c * P:(c + 1) * P], [(h2[:, g.s, c * P:(c + 1) * P], s_sums[:, g.s, 2:2 + N])])
                mm.then_inc(sh_done, 1)

            def l2_hidden(g):
                first_use(pe, g, part_split["w1"], 1)
                wait(pe, x3_done, g.n)
                pe.wait_ge(sh_split, g.n + 1)
                by_weight(B2[:, 0:H], sh_hi, sh_lo, w1, FC).then_inc(w1_done, 1)

            def l2_smooth_hidden(g):
                pe.wait_ge(zn_done, g.n + 1)
                for c in range(HC):
                    mm = group(A2[:, c * P:(c + 1) * P], [(zn[:, c * P:(c + 1) * P], s_sums[:, g.s, 2:2 + N])])
                mm.then_inc(sz_done, 1)

            def l2_out(g):
                first_use(pe, g, part_split["w2"], 1)
                pe.wait_ge(sz_split, g.n + 1)
                by_weight(B2[:, 0:F], sz_hi, sz_lo, w2, HC).then_inc(w2_done, 1)

            def h3_transposes(g):
                first_use(pe, g, mv_filled, 1)
                pe.wait_ge(h3_done, g.n + 1)
                wait(pe, e_row_done, g.n)
                for c in range(FC):
                    mm = pe.transpose(A3[:, c * P:(c + 1) * P], h3[:, g.s2, c * P:(c + 1) * P], ident[:])
                mm.then_inc(h3_transposed, 1)

            def l3_aggregate(g):
                pe.wait_ge(h3_split, g.n + 1)
                group(A3[:, 0:F], [(adjm_t[:, g.s, :], h3[:, g.s2, :])]).then_inc(agg3_done, 1)

            def l3_products(g):
                first_use(pe, g, part_split["mv"], 1)
                first_use(pe, g, w2_scaled, 1)
                pe.wait_ge(h3_split, g.n + 1)
                wait(pe, y_done, g.n)
                by_weight(B3[:, :], h3t_hi, h3t_lo, mv, FC).then_inc(tv_done, 1)

            def l3_spread(g):
                pe.wait_ge(w_done, g.n + 1)
                pe.transpose(A3[:, 0:N], w_col[:].to_broadcast([P, N]), ident[:]).then_inc(w_spread, 1)

            def step(t, k):
                for piece, back in ((l1_hop2, 3), (l3_products, 6), (h1_transposes, 2), (l0_gates, 1),
                    (l0_incidence, 1), (l3_aggregate, 6), (l1_product2, 2), (l0_aggregate, 1),
                    (l2_smooth_hidden, 4), (l1_spread, 2), (l3_spread, 6), (l1_products10, 2),
                    (l2_smooth, 3), (l2_out, 4), (l1_transpose, 2), (l0_transposes, 0),
                    (h3_transposes, 5), (l1_hop1, 2), (l2_hidden, 3)):
                    if (g := in_flight(t, k, back, G)):
                        piece(g)

            run_steps(pe, step, G, (lambda: None, setup_layer1, setup_out))


def kernel(x, adj, nodemask, L0_gnn_W, L1_gnn_Wv, L1_gnn_bv, L1_gnn_aw, L1_gnn_ab, L1_gnn_Wk, L1_gnn_bk,
           L2_gnn_W1, L2_gnn_b1, L2_gnn_gamma, L2_gnn_beta, L2_gnn_W2, L2_gnn_b2, L3_gnn_Wqk, L3_gnn_Wv):
    import numpy as np
    import concourse.bacc as bacc
    from concourse.bass_utils import run_bass_kernel_spmd

    def columns(v):
        v = np.asarray(v)
        return v.reshape(-1, P).T

    aw = np.asarray(L1_gnn_aw).reshape(2, -1, P).transpose(2, 1, 0)
    arrays = {
        "x": x, "adj": adj, "adj_tr": np.asarray(adj).transpose(0, 2, 1),
        "mask_t": np.asarray(nodemask).T, "w0t": np.asarray(L0_gnn_W).T,
        "wk": L1_gnn_Wk, "w1t": np.asarray(L2_gnn_W1).T, "w2t": np.asarray(L2_gnn_W2).T,
        "wv3": L3_gnn_Wv, "wqk_t": np.asarray(L3_gnn_Wqk).T, "wv1t": np.asarray(L1_gnn_Wv).T,
        "aw": aw, "bv": columns(L1_gnn_bv), "ab": L1_gnn_ab, "bk": L1_gnn_bk, "b1": L2_gnn_b1,
        "b2": L2_gnn_b2, "gamma": columns(L2_gnn_gamma), "beta": columns(L2_gnn_beta),
    }
    arrays = {n: np.ascontiguousarray(a) for n, a in arrays.items()}
    nc = bacc.Bacc("TRN2", target_bir_lowering=False, num_devices=1)
    args = {n: nc.dram_tensor(n, a.shape, mybir.dt.from_np(a.dtype), kind="ExternalInput").ap()
            for n, a in arrays.items()}
    out = nc.dram_tensor("out", arrays["x"].shape, F32, kind="ExternalOutput").ap()
    build(nc, out=out, **args)
    r = run_bass_kernel_spmd(nc, [arrays], core_ids=[0])
    return r.results[0]["out"]
```
